# Optimizing a Trainium2 kernel written in Bass

```python
import numpy as np
import jax
import jax.numpy as jnp

def _softmax(x, axis=-1):
    return jax.nn.softmax(x, axis=axis)

def _gelu(x):
    return jax.nn.gelu(x, approximate=True)

def _silu(x):
    return jax.nn.silu(x)

def _sigmoid(x):
    return jax.nn.sigmoid(x)

def _layernorm(x, axis=-1, eps=1e-05):
    m = jnp.mean(x, axis=axis, keepdims=True)
    v = jnp.var(x, axis=axis, keepdims=True)
    return (x - m) / jnp.sqrt(v + eps)

def _scatter_add(tgt, idx, src, axis=0):
    return tgt.at[idx].add(src)

def _segment_sum(src, seg, n):
    return jax.ops.segment_sum(src, seg, n)
kernel_name = 'mk_adj_resnorm_d2_adj_r2_a765ba'

def setup_inputs(seed: int=0):
    np.random.seed(seed)
    _w = jnp.asarray

    def _rec_inputs():
        import jax
        import jax.numpy as jnp
        _gk = jax.random.key(seed)
        x = -0.0005207 + 1.001 * jax.random.normal(jax.random.fold_in(_gk, 1), (2048, 256), jnp.float32)
        _w = (1.0 + jnp.arange(2048, dtype=jnp.float32)) ** (-0.5)
        _w = _w / _w.mean()
        _pij = jnp.clip(0.00195312 * _w[:, None] * _w[None, :], 0.0, 1.0)
        _a = jax.random.uniform(jax.random.fold_in(_gk, 2), (2048, 2048)) < _pij
        adj = _a.astype(jnp.int32)
        return (x, adj)
    x, adj = _rec_inputs()

    def _L0_gnn_setup():
        import jax, jax.numpy as jnp
        import numpy as np
        HEAD_SIZE = 8
        QK_DIM = 256
        V_DIM = 256
        N = 2048
        ATT_DIM = QK_DIM // HEAD_SIZE
        SCALE = ATT_DIM ** (-0.5)
        NEG_FILL = jnp.float32(-9000000000000000.0)
        key = jax.random.key(seed)
        k1, k2, k3, k4 = jax.random.split(key, 4)
        x1 = jax.random.normal(k1, (N, QK_DIM), dtype=jnp.float32)
        x2 = jax.random.normal(k2, (N, QK_DIM), dtype=jnp.float32)
        v = jax.random.normal(k3, (N, V_DIM), dtype=jnp.float32)
        adj = jax.random.randint(k4, (N, N), 0, 2, dtype=jnp.int32)
        return {'x1': x1, 'x2': x2, 'v': v, 'adj': adj}
    _L0_gnn_all = _L0_gnn_setup()
    _L0_gnn_in = {k: v for k, v in _L0_gnn_all.items() if k in ('x2', 'v')}
    del _L0_gnn_all

    def _L1_gnn_setup():
        import jax, jax.numpy as jnp
        import numpy as np
        B, IN_F, OUT_F, H = (1024, 256, 256, 8)
        D = OUT_F // H
        key = jax.random.key(seed)
        ks = jax.random.split(key, 4)
        x = jax.random.normal(ks[0], (B, IN_F), dtype=jnp.float32)
        W_w = jax.random.normal(ks[1], (OUT_F, IN_F), dtype=jnp.float32) * (1.0 / np.sqrt(IN_F))
        W_b = jnp.zeros((OUT_F,), dtype=jnp.float32)
        a = jax.random.normal(ks[2], (2 * D, 1), dtype=jnp.float32) * 0.1
        adj = jax.random.randint(ks[3], (B, B), 0, 2, dtype=jnp.int32)
        return {'x': x, 'adj': adj, 'W_w': W_w, 'W_b': W_b, 'a': a}
    _L1_gnn_all = _L1_gnn_setup()
    _L1_gnn_in = {k: v for k, v in _L1_gnn_all.items() if k in ('W_w', 'W_b', 'a')}
    del _L1_gnn_all
    return {'x': x, 'adj': adj, 'L0_gnn_x2': _L0_gnn_in['x2'], 'L0_gnn_v': _L0_gnn_in['v'], 'L1_gnn_W_w': _L1_gnn_in['W_w'], 'L1_gnn_W_b': _L1_gnn_in['W_b'], 'L1_gnn_a': _L1_gnn_in['a']}

def reference(x, adj, L0_gnn_x2, L0_gnn_v, L1_gnn_W_w, L1_gnn_W_b, L1_gnn_a):
    import jax
    import jax.numpy as jnp

    def _L0_gnn_ref(x1, x2, v, adj):
        import jax, jax.numpy as jnp
        import numpy as np
        HEAD_SIZE = 8
        QK_DIM = 256
        V_DIM = 256
        N = 2048
        ATT_DIM = QK_DIM // HEAD_SIZE
        SCALE = ATT_DIM ** (-0.5)
        NEG_FILL = jnp.float32(-9000000000000000.0)
        n = x1.shape[0]
        q = x1.reshape(n, HEAD_SIZE, -1).transpose(1, 0, 2) * SCALE
        k = x2.reshape(n, HEAD_SIZE, -1).transpose(1, 0, 2)
        vv = v.reshape(n, HEAD_SIZE, -1).transpose(1, 0, 2)
        scores = jnp.einsum('hnd,hmd->hnm', q, k)
        scores = jnp.where(adj > 0, scores, NEG_FILL)
        attn = jax.nn.softmax(scores, axis=-1)
        out = jnp.einsum('hnm,hmd->hnd', attn, vv)
        return out.transpose(1, 0, 2).reshape(n, -1)

    def _L1_gnn_ref(x, adj, W_w, W_b, a):
        import jax, jax.numpy as jnp
        import numpy as np
        B, IN_F, OUT_F, H = (1024, 256, 256, 8)
        D = OUT_F // H
        Bn = x.shape[0]
        h = (x @ W_w.T + W_b).reshape(Bn, H, D)
        a_src, a_dst = (a[:D, 0], a[D:, 0])
        s_src = jnp.einsum('bhd,d->bh', h, a_src)
        s_dst = jnp.einsum('bhd,d->bh', h, a_dst)
        e = jax.nn.leaky_relu(s_src[:, None, :] + s_dst[None, :, :], negative_slope=0.2)
        e = jnp.where(adj[:, :, None] == 0, jnp.float32(-1000000000.0), e)
        attn = jax.nn.softmax(e, axis=1)
        h_prime = jnp.einsum('ijh,jhd->ihd', attn, h).reshape(Bn, H * D)
        return jax.nn.elu(h_prime)
    x = _layernorm(x + _L0_gnn_ref(x, L0_gnn_x2, L0_gnn_v, adj), axis=-1)
    x = _layernorm(x + _L1_gnn_ref(x, adj, L1_gnn_W_w, L1_gnn_W_b, L1_gnn_a), axis=-1)
    return x

_drawn_inputs = setup_inputs


def setup_inputs(seed=0):
    import zlib

    import numpy as np

    out = dict(_drawn_inputs(seed))
    spreads = {'L1_gnn_W_b': (0.0, 0.1)}
    factors = {}
    for name, (base, spread) in spreads.items():
        noise = np.random.default_rng([zlib.crc32(name.encode()), seed]).standard_normal(out[name].shape)
        drawn = base * np.exp(spread * noise) if base else spread * noise
        out[name] = jnp.asarray(drawn.astype(out[name].dtype))
    for name, factor in factors.items():
        out[name] = (out[name] * factor).astype(out[name].dtype)
    return out
```

```python
from contextlib import ExitStack

import concourse.bass as bass
from concourse import mybir

F32 = mybir.dt.float32
I32 = mybir.dt.int32
ALU = mybir.AluOpType
ACT = mybir.ActivationFunctionType
AX_X = mybir.AxisListType.X
ts = bass.ts

P = 128
H = 8
SLOPE = 0.2
EPS = 1e-5
NEG0 = 9000000000000000.0
NEG1 = 1000000000.0
STEPS = (1 + 3 * H + 5, 1 + 5 * H + 8)
ELU_AT = 1 + 5 * H + 1


class Steps:

    def __init__(self, eng, sem, base=0):
        self.eng, self.sem, self.base, self.n = eng, sem, base, 0

    def did(self, ins):
        ins.then_inc(self.sem, 1)
        self.n += 1

    def wait(self):
        self.eng.wait_ge(self.sem, self.base + self.n)


def resnorm_gnn(nc, x, xT, adj, kT, v, wT, w_b, a, out, sdT_dram):
    N, C = x.shape
    D = C // H
    NT = N // P
    NB = N // 512
    SCALE = float(D) ** -0.5

    with ExitStack() as ctx:
        def sb(name, shape, dt=F32):
            return ctx.enter_context(nc.sbuf_tensor(name, shape, dt))

        def psum(name, shape):
            return ctx.enter_context(nc.psum_tensor(name, shape, F32))

        def sem(name):
            return ctx.enter_context(nc.semaphore(name))

        ident = sb("ident", [P, P])
        ones_row = sb("ones_row", [1, P])
        big = sb("big", [P, H, N])
        val = sb("val", [P, NT, C])
        res = sb("res", [P, NT, C])
        q_tile = sb("q_tile", [D, H, P])
        adj_tile = sb("adj_tile", [P, N], I32)
        mask = sb("mask", [P, N])
        fill = sb("fill", [P, N])
        score = sb("score", [P, N])
        prob = sb("prob", [P, N])
        probT = sb("probT", [P, NT, P])
        att = sb("att", [P, C])
        neg_part = sb("neg_part", [P, C])
        nmax = sb("nmax", [P, 1])
        rsum = sb("rsum", [P, 1])
        rinv = sb("rinv", [P, 1])
        mean = sb("mean", [P, 1])
        var = sb("var", [P, NT])
        std = sb("std", [P, NT])
        rstd = sb("rstd", [P, NT])
        wT_sb = sb("wT_sb", [P, 2, C])
        bias_row = sb("bias_row", [1, C])
        a_b = sb("a_b", [P, 2 * D])
        xt_sb = sb("xt_sb", [P, 2, P])
        ssrc = sb("ssrc", [P, NT, H])
        sdst = sb("sdst", [P, NT, H])
        sdT = sb("sdT", [H, N])

        ps_s = psum("ps_s", [P, N])
        ps_t = psum("ps_t", [P, 2, 512])
        ps_o = psum("ps_o", [P, 512])
        ps_m = psum("ps_m", [P, 512])

        const_ready = sem("const_ready")
        loaded = sem("loaded")
        layer1_loaded = sem("layer1_loaded")
        names = ["adj_loaded", "q_loaded", "adj_used", "q_used", "scores_ready", "scores_read", "pre_ready", "max_ready",
                 "probs_ready", "turned", "turn_copied", "summed", "att_ready", "exp_ready", "step", "var_ready", "std_ready"]
        S = [{n: sem(f"{n}{layer}") for n in names} for layer in range(2)]
        norm_ready = sem("norm_ready")
        xt_ready = sem("xt_ready")
        xt_copied = sem("xt_copied")
        h_ready = sem("h_ready")
        h_copied = sem("h_copied")
        hstep = sem("hstep")
        sd_turned = sem("sd_turned")
        sd_copied = sem("sd_copied")
        sd_stored = sem("sd_stored")
        out_done = sem("out_done")

        block = ctx.enter_context(nc.Block())

        @block.sync
        def _(sp):
            sp.dma_start(big[0:D, :, :], kT.rearrange("(h d) n -> d h n", d=D)).then_inc(loaded, 16)
            sp.dma_start(val[:], v.rearrange("(t p) c -> p t c", p=P)).then_inc(loaded, 16)
            sp.dma_start(res[:], x.rearrange("(t p) c -> p t c", p=P)).then_inc(loaded, 16)
            sp.dma_start(wT_sb[:], wT.rearrange("(k p) c -> p k c", p=P)).then_inc(loaded, 16)
            sp.dma_start(bias_row[:], w_b.rearrange("(a c) -> a c", a=1)).then_inc(loaded, 16)
            sp.dma_start(a_b[:], a.rearrange("k b -> b k").to_broadcast([P, 2 * D])).then_inc(loaded, 16)
            sp.wait_ge(sd_copied, NT)
            sp.wait_ge(norm_ready, 1)
            sp.dma_start(sdT_dram, sdT[:]).then_inc(sd_stored, 16)
            sp.wait_ge(sd_stored, 16)
            sp.dma_start(big[:], sdT_dram.rearrange("(a h) n -> a h n", a=1).to_broadcast([P, H, N])).then_inc(layer1_loaded, 16)
            sp.wait_ge(norm_ready, 2)
            sp.dma_start(out.rearrange("(t p) c -> p t c", p=P), res[:]).then_inc(out_done, 16)
            sp.wait_ge(out_done, 16)

        @block.gpsimd
        def _(pool):
            nc.gpsimd.memset(ident[:], 0.0).then_inc(const_ready, 1)
            pool.wait_ge(const_ready, 1)
            nc.gpsimd.affine_select(out=ident[:], in_=ident[:], compare_op=ALU.not_equal, fill=1.0, base=0,
                                    pattern=[[-1, P]], channel_multiplier=1).then_inc(const_ready, 1)
            nc.gpsimd.memset(ones_row[:], 1.0).then_inc(const_ready, 1)
            for layer in range(2):
                s = S[layer]
                if layer == 1:
                    pool.wait_ge(S[0]["adj_used"], NT + 1)
                with pool.Fori(0, NT) as t:
                    pool.wait_ge(s["adj_used"], t + 1)
                    pool.dma_start(adj_tile[:], adj[ts(t, P), :]).then_inc(s["adj_loaded"], 16)
                    if layer == 0:
                        pool.wait_ge(s["q_used"], t + 1)
                        pool.dma_start(q_tile[:], xT[:, ts(t, P)].rearrange("(h d) n -> d h n", d=D)).then_inc(s["q_loaded"], 16)

        @block.tensor
        def _(pe):
            pe.wait_ge(const_ready, 3)
            pe.wait_ge(loaded, 96)
            for layer in range(2):
                s = S[layer]
                for name in ("turned", "summed"):
                    pe.sem_inc(s[name], 1)
                if layer == 1:
                    pe.wait_ge(norm_ready, 1)
                    for t in range(NT):
                        if t >= 1:
                            pe.wait_ge(xt_copied, t)
                        for k in range(2):
                            last = nc.tensor.transpose(ps_t[:, 0, k * P:(k + 1) * P], res[:, t, k * P:(k + 1) * P], ident[:])
                        last.then_inc(xt_ready, 1)
                        pe.wait_ge(xt_copied, t + 1)
                        if t >= 1:
                            pe.wait_ge(h_copied, t)
                        for k in range(2):
                            nc.tensor.matmul(ps_m[:, 0:C], xt_sb[:, k, :], wT_sb[:, k, :], start=(k == 0), stop=False)
                        nc.tensor.matmul(ps_m[:, 0:C], ones_row[:], bias_row[:], start=False, stop=True).then_inc(h_ready, 1)
                    for t in range(NT):
                        pe.wait_ge(hstep, 4 * (t + 1))
                        if t >= 1:
                            pe.wait_ge(sd_copied, t)
                        nc.tensor.transpose(ps_o[0:H, 0:P], sdst[:, t, :], ident[:]).then_inc(sd_turned, 1)
                    pe.wait_ge(sd_copied, NT)
                with pe.Fori(0, NT) as t:
                    for h in range(H):
                        n = t * H + h
                        if layer == 0:
                            if h == 0:
                                pe.wait_ge(s["q_loaded"], 16 * t + 16)
                            pe.wait_ge(s["scores_read"], n + 1)
                            for b in range(NB):
                                last = nc.tensor.matmul(ps_s[:, ts(b, 512)], q_tile[:, h, :], big[0:D, h, ts(b, 512)], start=True, stop=True)
                            last.then_inc(s["scores_ready"], 1)
                        pe.wait_ge(s["probs_ready"], n + 2)
                        for g in range(NT // 4):
                            pe.wait_ge(s["turn_copied"], 4 * n + max(g - 1, 0) + 1)
                            for j in range(4):
                                last = nc.tensor.transpose(ps_t[:, g % 2, ts(j, P)], prob[:, ts(4 * g + j, P)], ident[:])
                            last.then_inc(s["turned"], 1)
                        pe.wait_ge(s["turn_copied"], 4 * n + 4 + 1)
                        if h == 0:
                            pe.wait_ge(s["att_ready"], t + 1)
                        for m in range(NT):
                            last = nc.tensor.matmul(ps_o[:, ts(h, D)], probT[:, m, :], val[:, m, ts(h, D)], start=(m == 0), stop=(m == NT - 1))
                        last.then_inc(s["summed"], 1)

        @block.scalar
        def _(act):
            for layer in range(2):
                s = S[layer]
                for name in ("turn_copied", "probs_ready"):
                    act.sem_inc(s[name], 1)
                if layer == 1:
                    for t in range(NT):
                        act.wait_ge(xt_ready, t + 1)
                        if t >= 1:
                            act.wait_ge(h_ready, t)
                        nc.scalar.copy(xt_sb[:].rearrange("p k n -> p (k n)"), ps_t[:, 0, 0:2 * P]).then_inc(xt_copied, 1)
                        act.wait_ge(h_ready, t + 1)
                        nc.scalar.copy(val[:, t, :], ps_m[:, 0:C]).then_inc(h_copied, 1)
                    for t in range(NT):
                        act.wait_ge(sd_turned, t + 1)
                        nc.scalar.copy(sdT[:, ts(t, P)], ps_o[0:H, 0:P]).then_inc(sd_copied, 1)
                    act.wait_ge(layer1_loaded, 16)
                with act.Fori(0, NT) as t:
                    for h in range(H):
                        n = t * H + h
                        if layer == 1:
                            act.wait_ge(s["turned"], 4 * n + 1)
                            nc.scalar.activation(prob[:], big[:, h, :], ACT.Identity, bias=ssrc[:, t, h:h + 1]).then_inc(s["pre_ready"], 1)
                        act.wait_ge(s["max_ready"], n + 1)
                        if layer == 0:
                            act.wait_ge(s["turned"], 4 * n + 1)
                        nc.scalar.activation(prob[:], score[:], ACT.Exp, bias=nmax[:], accum_out=rsum[:]).then_inc(s["probs_ready"], 1)
                        for g in range(NT // 4):
                            act.wait_ge(s["turned"], 4 * n + g + 2)
                            if g == 0:
                                act.wait_ge(s["summed"], n + 1)
                            nc.scalar.copy(probT[:, ts(g, 4), :].rearrange("p m r -> p (m r)"), ps_t[:, g % 2, :]).then_inc(s["turn_copied"], 1)
                    if layer == 1:
                        act.wait_ge(s["step"], STEPS[1] * t + ELU_AT + 1)
                        nc.scalar.activation(neg_part[:], neg_part[:], ACT.Exp).then_inc(s["exp_ready"], 1)
                act.wait_ge(s["var_ready"], 1)
                nc.scalar.activation(std[:], std[:], ACT.Sqrt).then_inc(s["std_ready"], 1)

        @block.vector
        def _(dve):
            dve.wait_ge(loaded, 96)
            for layer in range(2):
                s = S[layer]
                for name in ("adj_used", "q_used", "scores_read", "att_ready", "step"):
                    dve.sem_inc(s[name], 1)
                if layer == 1:
                    hs = Steps(dve, hstep)
                    for t in range(NT):
                        dve.wait_ge(h_copied, t + 1)
                        for k, dst in ((0, ssrc), (1, sdst)):
                            hs.wait()
                            hs.did(nc.vector.tensor_tensor(att[:].rearrange("p (h d) -> p h d", d=D), val[:, t, :].rearrange("p (h d) -> p h d", d=D),
                                                           a_b[:, k * D:(k + 1) * D].unsqueeze(1).to_broadcast([P, H, D]), ALU.mult))
                            hs.wait()
                            hs.did(nc.vector.tensor_reduce(dst[:, t, :], att[:].rearrange("p (h d) -> p h d", d=D), AX_X, ALU.add))
                with dve.Fori(0, NT) as t:
                    st = Steps(dve, s["step"], STEPS[layer] * t + 1)
                    dve.wait_ge(s["adj_loaded"], 16 * (t + 1))
                    st.wait()
                    nc.vector.tensor_scalar(mask[:], adj_tile[:], 0.0, None, ALU.is_gt if layer == 0 else ALU.not_equal).then_inc(s["adj_used"], 1)
                    dve.wait_ge(s["adj_used"], t + 2)
                    st.did(nc.vector.tensor_scalar(fill[:], mask[:], -1.0, NEG0 if layer == 0 else NEG1, ALU.add, ALU.mult))
                    for h in range(H):
                        n = t * H + h
                        dve.wait_ge(s["probs_ready"], n + 1)
                        if layer == 0:
                            dve.wait_ge(s["scores_ready"], n + 1)
                            nc.vector.scalar_tensor_tensor(out=score[:], in0=ps_s[:], scalar=SCALE, in1=mask[:], op0=ALU.mult, op1=ALU.mult).then_inc(s["scores_read"], 1)
                            dve.wait_ge(s["scores_read"], n + 2)
                        else:
                            dve.wait_ge(s["pre_ready"], n + 1)
                            st.did(nc.vector.scalar_tensor_tensor(out=score[:], in0=prob[:], scalar=SLOPE, in1=prob[:], op0=ALU.mult, op1=ALU.max))
                            st.wait()
                            st.did(nc.vector.tensor_tensor(score[:], score[:], mask[:], ALU.mult))
                        st.wait()
                        st.did(nc.vector.tensor_tensor(score[:], score[:], fill[:], ALU.add))
                        st.wait()
                        nc.vector.tensor_reduce(nmax[:], score[:], AX_X, ALU.max, negate=True).then_inc(s["max_ready"], 1)
                        dve.wait_ge(s["probs_ready"], n + 2)
                        st.did(nc.vector.reciprocal(rinv[:], rsum[:]))
                        st.wait()
                        dve.wait_ge(s["summed"], n + 2)
                        st.did(nc.vector.tensor_scalar(att[:, ts(h, D)], ps_o[:, ts(h, D)], rinv[:], None, ALU.mult))
                    st.wait()
                    if layer == 0:
                        nc.vector.tensor_copy(mean[:], rinv[:]).then_inc(s["q_used"], 1)
                        dve.wait_ge(s["q_used"], t + 2)
                    if layer == 1:
                        st.did(nc.vector.tensor_scalar(neg_part[:], att[:], 0.0, None, ALU.min))
                        assert st.n == ELU_AT
                        dve.wait_ge(s["exp_ready"], t + 1)
                        st.did(nc.vector.tensor_scalar(neg_part[:], neg_part[:], -1.0, None, ALU.add))
                        st.wait()
                        st.did(nc.vector.scalar_tensor_tensor(out=att[:], in0=att[:], scalar=0.0, in1=neg_part[:], op0=ALU.max, op1=ALU.add))
                        st.wait()
                    st.did(nc.vector.tensor_tensor(att[:], res[:, t, :], att[:], ALU.add))
                    st.wait()
                    st.did(nc.vector.tensor_reduce(mean[:], att[:], AX_X, ALU.add))
                    st.wait()
                    st.did(nc.vector.tensor_scalar(mean[:], mean[:], 1.0 / C, None, ALU.mult))
                    st.wait()
                    st.did(nc.vector.tensor_scalar(res[:, t, :], att[:], mean[:], None, ALU.subtract))
                    st.wait()
                    st.did(nc.vector.tensor_tensor(att[:], res[:, t, :], res[:, t, :], ALU.mult))
                    st.wait()
                    nc.vector.tensor_reduce(var[:, ts(t, 1)], att[:], AX_X, ALU.add).then_inc(s["att_ready"], 1)
                    dve.wait_ge(s["att_ready"], t + 2)
                    assert st.n == STEPS[layer]
                st = Steps(dve, s["step"], STEPS[layer] * NT + 1)
                nc.vector.tensor_scalar(std[:], var[:], 1.0 / C, EPS, ALU.mult, ALU.add).then_inc(s["var_ready"], 1)
                dve.wait_ge(s["std_ready"], 1)
                st.did(nc.vector.reciprocal(rstd[:], std[:]))
                st.wait()
                for t in range(NT):
                    last = nc.vector.tensor_scalar(res[:, t, :], res[:, t, :], rstd[:, t:t + 1], None, ALU.mult)
                last.then_inc(norm_ready, 1)


def kernel(x, adj, L0_gnn_x2, L0_gnn_v, L1_gnn_W_w, L1_gnn_W_b, L1_gnn_a):
    import numpy as np
    import concourse.bacc as bacc
    from concourse.bass_utils import run_bass_kernel_spmd

    nc = bacc.Bacc("TRN2", target_bir_lowering=False, num_devices=1)
    x, x2, w = (np.asarray(t) for t in (x, L0_gnn_x2, L1_gnn_W_w))
    laid_out = {
        "x": x, "xT": x.T, "adj": adj, "kT": x2.T, "v": L0_gnn_v,
        "wT": w.T, "w_b": L1_gnn_W_b, "a": L1_gnn_a,
    }
    arrays, args = {}, []
    for name, arr in laid_out.items():
        arr = np.ascontiguousarray(arr)
        arrays[f"in_{name}"] = arr
        args.append(nc.dram_tensor(f"in_{name}", arr.shape, mybir.dt.from_np(arr.dtype), kind="ExternalInput").ap())
    args.append(nc.dram_tensor("out_0", x.shape, F32, kind="ExternalOutput").ap())
    args.append(nc.dram_tensor("sdT_dram", (H, x.shape[0]), F32, kind="Internal").ap())
    resnorm_gnn(nc, *args)
    return run_bass_kernel_spmd(nc, [arrays], core_ids=[0]).results[0]["out_0"]
```

```python
from contextlib import ExitStack

import concourse.bass as bass
from concourse import mybir

F32 = mybir.dt.float32
BF16 = mybir.dt.bfloat16
I32 = mybir.dt.int32
ALU = mybir.AluOpType
ACT = mybir.ActivationFunctionType
AX_X = mybir.AxisListType.X
ts = bass.ts

P = 128
H = 8
SLOPE = 0.2
EPS = 1e-5
NEG0 = 9000000000000000.0
NEG1 = 1000000000.0
STEPS = (1 + 3 * H + 5, 1 + 5 * H + 8)
ELU_AT = 1 + 5 * H + 1

BIG = 1e30
TOP = 8
QUARTER = 512
SCAN = 16
RING = 20

CHUNKS = (17, 8, 6, 5, 5, 5, 4, 4, 4, 4, 3, 3, 3, 3, 3, 3)
SEGMENTS = (4, 4, 4, 4) + (2,) * 12
ROUNDS = (2,) + (1,) * 15
ORDER = (15, 0, 14, 1, 13, 2, 12, 3, 11, 4, 10, 5, 9, 6, 8, 7)


class Steps:

    def __init__(self, eng, sem, base=0):
        self.eng, self.sem, self.base, self.n = eng, sem, base, 0

    def did(self, ins):
        ins.then_inc(self.sem, 1)
        self.n += 1

    def wait(self):
        self.eng.wait_ge(self.sem, self.base + self.n)




class Plan:

    def __init__(self):
        self.first, self.batches, self.batch0, self.rounds, self.round0, self.scans, self.scan0 = {}, {}, {}, {}, {}, {}, {}
        q = b = r = g = 0
        for t in ORDER:
            C = CHUNKS[t]
            self.first[t] = q
            pairs, c = [], 0
            while c < C:
                n = 2 if c + 1 < C and (q + c) % RING != RING - 1 else 1
                pairs.append((c, n))
                c += n
            self.batches[t], self.batch0[t] = pairs, b
            b += len(pairs)
            per = max(1, 512 // (2 * self.slots(t)))
            self.rounds[t] = [(c, min(per, C - c)) for c in range(0, C, per)]
            self.round0[t] = r
            r += len(self.rounds[t])
            n = -(-C // SCAN)
            per = -(-C // n)
            self.scans[t] = [(c, min(per, C - c)) for c in range(0, C, per)]
            self.scan0[t] = g
            g += n
            q += C
        self.n_chunks, self.n_batches, self.n_rounds, self.n_scans = q, b, r, g
        assert q % RING == 0

    def slots(self, t):
        return 4 * SEGMENTS[t] * ROUNDS[t] * TOP


def general_pass(nc, x, xT, adj, kT, v, wT, w_b, a, out, sdT_dram, needed):
    N, C = x.shape
    D = C // H
    NT = N // P
    NB = N // 512
    SCALE = float(D) ** -0.5

    with ExitStack() as ctx:
        def sb(name, shape, dt=F32):
            return ctx.enter_context(nc.sbuf_tensor(name, shape, dt))

        def psum(name, shape):
            return ctx.enter_context(nc.psum_tensor(name, shape, F32))

        def sem(name):
            return ctx.enter_context(nc.semaphore(name))

        ident = sb("ident", [P, P])
        ones_row = sb("ones_row", [1, P])
        big = sb("big", [P, H, N])
        val = sb("val", [P, NT, C])
        res = sb("res", [P, NT, C])
        q_tile = sb("q_tile", [D, H, P])
        adj_tile = sb("adj_tile", [P, N], I32)
        mask = sb("mask", [P, N])
        fill = sb("fill", [P, N])
        score = sb("score", [P, N])
        prob = sb("prob", [P, N])
        probT = sb("probT", [P, NT, P])
        att = sb("att", [P, C])
        neg_part = sb("neg_part", [P, C])
        nmax = sb("nmax", [P, 1])
        rsum = sb("rsum", [P, 1])
        rinv = sb("rinv", [P, 1])
        mean = sb("mean", [P, 1])
        var = sb("var", [P, NT])
        std = sb("std", [P, NT])
        rstd = sb("rstd", [P, NT])
        wT_sb = sb("wT_sb", [P, 2, C])
        bias_row = sb("bias_row", [1, C])
        a_b = sb("a_b", [P, 2 * D])
        xt_sb = sb("xt_sb", [P, 2, P])
        ssrc = sb("ssrc", [P, NT, H])
        sdst = sb("sdst", [P, NT, H])
        sdT = sb("sdT", [H, N])

        ps_s = psum("ps_s", [P, N])
        ps_t = psum("ps_t", [P, 2, 512])
        ps_o = psum("ps_o", [P, 512])
        ps_m = psum("ps_m", [P, 512])

        const_ready = sem("const_ready")
        loaded = sem("loaded")
        layer1_loaded = sem("layer1_loaded")
        names = ["adj_loaded", "q_loaded", "adj_used", "q_used", "scores_ready", "scores_read", "pre_ready", "max_ready",
                 "probs_ready", "turned", "turn_copied", "summed", "att_ready", "exp_ready", "step", "var_ready", "std_ready"]
        S = [{n: sem(f"{n}{layer}") for n in names} for layer in range(2)]
        norm_ready = sem("norm_ready")
        xt_ready = sem("xt_ready")
        xt_copied = sem("xt_copied")
        h_ready = sem("h_ready")
        h_copied = sem("h_copied")
        hstep = sem("hstep")
        sd_turned = sem("sd_turned")
        sd_copied = sem("sd_copied")
        sd_stored = sem("sd_stored")
        out_done = sem("out_done")

        block = ctx.enter_context(nc.Block())

        @block.sync
        def _(sp):
            with sp.If(sp.value_load(needed, min_val=0, max_val=1) > 0):
                sp.dma_start(big[0:D, :, :], kT.rearrange("(h d) n -> d h n", d=D)).then_inc(loaded, 16)
                sp.dma_start(val[:], v.rearrange("(t p) c -> p t c", p=P)).then_inc(loaded, 16)
                sp.dma_start(res[:], x.rearrange("(t p) c -> p t c", p=P)).then_inc(loaded, 16)
                sp.dma_start(wT_sb[:], wT.rearrange("(k p) c -> p k c", p=P)).then_inc(loaded, 16)
                sp.dma_start(bias_row[:], w_b.rearrange("(a c) -> a c", a=1)).then_inc(loaded, 16)
                sp.dma_start(a_b[:], a.rearrange("k b -> b k").to_broadcast([P, 2 * D])).then_inc(loaded, 16)
                sp.wait_ge(sd_copied, NT)
                sp.wait_ge(norm_ready, 1)
                sp.dma_start(sdT_dram, sdT[:]).then_inc(sd_stored, 16)
                sp.wait_ge(sd_stored, 16)
                sp.dma_start(big[:], sdT_dram.rearrange("(a h) n -> a h n", a=1).to_broadcast([P, H, N])).then_inc(layer1_loaded, 16)
                sp.wait_ge(norm_ready, 2)
                sp.dma_start(out.rearrange("(t p) c -> p t c", p=P), res[:]).then_inc(out_done, 16)
                sp.wait_ge(out_done, 16)

        @block.gpsimd
        def _(pool):
            with pool.If(pool.value_load(needed, min_val=0, max_val=1) > 0):
                nc.gpsimd.memset(ident[:], 0.0).then_inc(const_ready, 1)
                pool.wait_ge(const_ready, 1)
                nc.gpsimd.affine_select(out=ident[:], in_=ident[:], compare_op=ALU.not_equal, fill=1.0, base=0,
                                        pattern=[[-1, P]], channel_multiplier=1).then_inc(const_ready, 1)
                nc.gpsimd.memset(ones_row[:], 1.0).then_inc(const_ready, 1)
                for layer in range(2):
                    s = S[layer]
                    if layer == 1:
                        pool.wait_ge(S[0]["adj_used"], NT + 1)
                    with pool.Fori(0, NT) as t:
                        pool.wait_ge(s["adj_used"], t + 1)
                        pool.dma_start(adj_tile[:], adj[ts(t, P), :]).then_inc(s["adj_loaded"], 16)
                        if layer == 0:
                            pool.wait_ge(s["q_used"], t + 1)
                            pool.dma_start(q_tile[:], xT[:, ts(t, P)].rearrange("(h d) n -> d h n", d=D)).then_inc(s["q_loaded"], 16)

        @block.tensor
        def _(pe):
            with pe.If(pe.value_load(needed, min_val=0, max_val=1) > 0):
                pe.wait_ge(const_ready, 3)
                pe.wait_ge(loaded, 96)
                for layer in range(2):
                    s = S[layer]
                    for name in ("turned", "summed"):
                        pe.sem_inc(s[name], 1)
                    if layer == 1:
                        pe.wait_ge(norm_ready, 1)
                        for t in range(NT):
                            if t >= 1:
                                pe.wait_ge(xt_copied, t)
                            for k in range(2):
                                last = nc.tensor.transpose(ps_t[:, 0, k * P:(k + 1) * P], res[:, t, k * P:(k + 1) * P], ident[:])
                            last.then_inc(xt_ready, 1)
                            pe.wait_ge(xt_copied, t + 1)
                            if t >= 1:
                                pe.wait_ge(h_copied, t)
                            for k in range(2):
                                nc.tensor.matmul(ps_m[:, 0:C], xt_sb[:, k, :], wT_sb[:, k, :], start=(k == 0), stop=False)
                            nc.tensor.matmul(ps_m[:, 0:C], ones_row[:], bias_row[:], start=False, stop=True).then_inc(h_ready, 1)
                        for t in range(NT):
                            pe.wait_ge(hstep, 4 * (t + 1))
                            if t >= 1:
                                pe.wait_ge(sd_copied, t)
                            nc.tensor.transpose(ps_o[0:H, 0:P], sdst[:, t, :], ident[:]).then_inc(sd_turned, 1)
                        pe.wait_ge(sd_copied, NT)
                    with pe.Fori(0, NT) as t:
                        for h in range(H):
                            n = t * H + h
                            if layer == 0:
                                if h == 0:
                                    pe.wait_ge(s["q_loaded"], 16 * t + 16)
                                pe.wait_ge(s["scores_read"], n + 1)
                                for b in range(NB):
                                    last = nc.tensor.matmul(ps_s[:, ts(b, 512)], q_tile[:, h, :], big[0:D, h, ts(b, 512)], start=True, stop=True)
                                last.then_inc(s["scores_ready"], 1)
                            pe.wait_ge(s["probs_ready"], n + 2)
                            for g in range(NT // 4):
                                pe.wait_ge(s["turn_copied"], 4 * n + max(g - 1, 0) + 1)
                                for j in range(4):
                                    last = nc.tensor.transpose(ps_t[:, g % 2, ts(j, P)], prob[:, ts(4 * g + j, P)], ident[:])
                                last.then_inc(s["turned"], 1)
                            pe.wait_ge(s["turn_copied"], 4 * n + 4 + 1)
                            if h == 0:
                                pe.wait_ge(s["att_ready"], t + 1)
                            for m in range(NT):
                                last = nc.tensor.matmul(ps_o[:, ts(h, D)], probT[:, m, :], val[:, m, ts(h, D)], start=(m == 0), stop=(m == NT - 1))
                            last.then_inc(s["summed"], 1)

        @block.scalar
        def _(act):
            with act.If(act.value_load(needed, min_val=0, max_val=1) > 0):
                for layer in range(2):
                    s = S[layer]
                    for name in ("turn_copied", "probs_ready"):
                        act.sem_inc(s[name], 1)
                    if layer == 1:
                        for t in range(NT):
                            act.wait_ge(xt_ready, t + 1)
                            if t >= 1:
                                act.wait_ge(h_ready, t)
                            nc.scalar.copy(xt_sb[:].rearrange("p k n -> p (k n)"), ps_t[:, 0, 0:2 * P]).then_inc(xt_copied, 1)
                            act.wait_ge(h_ready, t + 1)
                            nc.scalar.copy(val[:, t, :], ps_m[:, 0:C]).then_inc(h_copied, 1)
                        for t in range(NT):
                            act.wait_ge(sd_turned, t + 1)
                            nc.scalar.copy(sdT[:, ts(t, P)], ps_o[0:H, 0:P]).then_inc(sd_copied, 1)
                        act.wait_ge(layer1_loaded, 16)
                    with act.Fori(0, NT) as t:
                        for h in range(H):
                            n = t * H + h
                            if layer == 1:
                                act.wait_ge(s["turned"], 4 * n + 1)
                                nc.scalar.activation(prob[:], big[:, h, :], ACT.Identity, bias=ssrc[:, t, h:h + 1]).then_inc(s["pre_ready"], 1)
                            act.wait_ge(s["max_ready"], n + 1)
                            if layer == 0:
                                act.wait_ge(s["turned"], 4 * n + 1)
                            nc.scalar.activation(prob[:], score[:], ACT.Exp, bias=nmax[:], accum_out=rsum[:]).then_inc(s["probs_ready"], 1)
                            for g in range(NT // 4):
                                act.wait_ge(s["turned"], 4 * n + g + 2)
                                if g == 0:
                                    act.wait_ge(s["summed"], n + 1)
                                nc.scalar.copy(probT[:, ts(g, 4), :].rearrange("p m r -> p (m r)"), ps_t[:, g % 2, :]).then_inc(s["turn_copied"], 1)
                        if layer == 1:
                            act.wait_ge(s["step"], STEPS[1] * t + ELU_AT + 1)
                            nc.scalar.activation(neg_part[:], neg_part[:], ACT.Exp).then_inc(s["exp_ready"], 1)
                    act.wait_ge(s["var_ready"], 1)
                    nc.scalar.activation(std[:], std[:], ACT.Sqrt).then_inc(s["std_ready"], 1)

        @block.vector
        def _(dve):
            with dve.If(dve.value_load(needed, min_val=0, max_val=1) > 0):
                dve.wait_ge(loaded, 96)
                for layer in range(2):
                    s = S[layer]
                    for name in ("adj_used", "q_used", "scores_read", "att_ready", "step"):
                        dve.sem_inc(s[name], 1)
                    if layer == 1:
                        hs = Steps(dve, hstep)
                        for t in range(NT):
                            dve.wait_ge(h_copied, t + 1)
                            for k, dst in ((0, ssrc), (1, sdst)):
                                hs.wait()
                                hs.did(nc.vector.tensor_tensor(att[:].rearrange("p (h d) -> p h d", d=D), val[:, t, :].rearrange("p (h d) -> p h d", d=D),
                                                               a_b[:, k * D:(k + 1) * D].unsqueeze(1).to_broadcast([P, H, D]), ALU.mult))
                                hs.wait()
                                hs.did(nc.vector.tensor_reduce(dst[:, t, :], att[:].rearrange("p (h d) -> p h d", d=D), AX_X, ALU.add))
                    with dve.Fori(0, NT) as t:
                        st = Steps(dve, s["step"], STEPS[layer] * t + 1)
                        dve.wait_ge(s["adj_loaded"], 16 * (t + 1))
                        st.wait()
                        nc.vector.tensor_scalar(mask[:], adj_tile[:], 0.0, None, ALU.is_gt if layer == 0 else ALU.not_equal).then_inc(s["adj_used"], 1)
                        dve.wait_ge(s["adj_used"], t + 2)
                        st.did(nc.vector.tensor_scalar(fill[:], mask[:], -1.0, NEG0 if layer == 0 else NEG1, ALU.add, ALU.mult))
                        for h in range(H):
                            n = t * H + h
                            dve.wait_ge(s["probs_ready"], n + 1)
                            if layer == 0:
                                dve.wait_ge(s["scores_ready"], n + 1)
                                nc.vector.scalar_tensor_tensor(out=score[:], in0=ps_s[:], scalar=SCALE, in1=mask[:], op0=ALU.mult, op1=ALU.mult).then_inc(s["scores_read"], 1)
                                dve.wait_ge(s["scores_read"], n + 2)
                            else:
                                dve.wait_ge(s["pre_ready"], n + 1)
                                st.did(nc.vector.scalar_tensor_tensor(out=score[:], in0=prob[:], scalar=SLOPE, in1=prob[:], op0=ALU.mult, op1=ALU.max))
                                st.wait()
                                st.did(nc.vector.tensor_tensor(score[:], score[:], mask[:], ALU.mult))
                            st.wait()
                            st.did(nc.vector.tensor_tensor(score[:], score[:], fill[:], ALU.add))
                            st.wait()
                            nc.vector.tensor_reduce(nmax[:], score[:], AX_X, ALU.max, negate=True).then_inc(s["max_ready"], 1)
                            dve.wait_ge(s["probs_ready"], n + 2)
                            st.did(nc.vector.reciprocal(rinv[:], rsum[:]))
                            st.wait()
                            dve.wait_ge(s["summed"], n + 2)
                            st.did(nc.vector.tensor_scalar(att[:, ts(h, D)], ps_o[:, ts(h, D)], rinv[:], None, ALU.mult))
                        st.wait()
                        if layer == 0:
                            nc.vector.tensor_copy(mean[:], rinv[:]).then_inc(s["q_used"], 1)
                            dve.wait_ge(s["q_used"], t + 2)
                        if layer == 1:
                            st.did(nc.vector.tensor_scalar(neg_part[:], att[:], 0.0, None, ALU.min))
                            assert st.n == ELU_AT
                            dve.wait_ge(s["exp_ready"], t + 1)
                            st.did(nc.vector.tensor_scalar(neg_part[:], neg_part[:], -1.0, None, ALU.add))
                            st.wait()
                            st.did(nc.vector.scalar_tensor_tensor(out=att[:], in0=att[:], scalar=0.0, in1=neg_part[:], op0=ALU.max, op1=ALU.add))
                            st.wait()
                        st.did(nc.vector.tensor_tensor(att[:], res[:, t, :], att[:], ALU.add))
                        st.wait()
                        st.did(nc.vector.tensor_reduce(mean[:], att[:], AX_X, ALU.add))
                        st.wait()
                        st.did(nc.vector.tensor_scalar(mean[:], mean[:], 1.0 / C, None, ALU.mult))
                        st.wait()
                        st.did(nc.vector.tensor_scalar(res[:, t, :], att[:], mean[:], None, ALU.subtract))
                        st.wait()
                        st.did(nc.vector.tensor_tensor(att[:], res[:, t, :], res[:, t, :], ALU.mult))
                        st.wait()
                        nc.vector.tensor_reduce(var[:, ts(t, 1)], att[:], AX_X, ALU.add).then_inc(s["att_ready"], 1)
                        dve.wait_ge(s["att_ready"], t + 2)
                        assert st.n == STEPS[layer]
                    st = Steps(dve, s["step"], STEPS[layer] * NT + 1)
                    nc.vector.tensor_scalar(std[:], var[:], 1.0 / C, EPS, ALU.mult, ALU.add).then_inc(s["var_ready"], 1)
                    dve.wait_ge(s["std_ready"], 1)
                    st.did(nc.vector.reciprocal(rstd[:], std[:]))
                    st.wait()
                    for t in range(NT):
                        last = nc.vector.tensor_scalar(res[:, t, :], res[:, t, :], rstd[:, t:t + 1], None, ALU.mult)
                    last.then_inc(norm_ready, 1)




def edge_pass(nc, x, adj, kv, w_nat, wT, w_b, a, out, table, needed):
    N, C = x.shape
    D = C // H
    NT = N // P
    CX = C + 2 * H
    CG = C + H
    SCALE = float(D) ** -0.5
    MAXC = max(CHUNKS)
    plan = Plan()

    with ExitStack() as ctx:
        def sb(name, shape, dt=F32):
            return ctx.enter_context(nc.sbuf_tensor(name, shape, dt))

        def psum(name, shape):
            return ctx.enter_context(nc.psum_tensor(name, shape, F32))

        def sem(name):
            return ctx.enter_context(nc.semaphore(name))

        ident = sb("e_ident", [P, P])
        ident2048 = sb("e_ident2048", [P, P], BF16)
        ones = sb("e_ones", [P, P])
        ones_bf = sb("e_ones_bf", [1, P], BF16)
        mean_w = sb("e_mean_w", [P, P])
        below = sb("e_below", [P, P])
        col_hi = sb("e_col_hi", [1, QUARTER // 64], BF16)
        col_lo = sb("e_col_lo", [1, 4, 64], BF16)
        edge_no = sb("e_edge_no", [P, MAXC * P])
        row_no1 = sb("e_row_no1", [P, P])
        edge_no1 = sb("e_edge_no1", [P, MAXC])
        chunk_at = sb("e_chunk_at", [P, MAXC + 1])
        is_tail = sb("e_is_tail", [P, 1])
        caps = sb("e_caps", [P, NT])
        part1 = sb("e_part1", [P, 1])
        eps = sb("e_eps", [P, 1])
        w_sb = sb("e_w", [P, 2, C])
        a_diag = sb("e_a_diag", [P, 2, 2 * H])
        w_ext = sb("e_w_ext", [P, 2, CX])
        b_row = sb("e_b_row", [1, CX])
        b_col = sb("e_b_col", [P, 2])
        res = sb("e_res", [P, NT, C])
        hx = sb("e_hx", [P, NT, CX])
        mean_row = sb("e_mean_row", [P, CG])
        adj_tile = sb("e_adj", [P, 2, N], I32)
        sgn = sb("e_sgn", [P, 2, N], BF16)
        slot = sb("e_slot", [P, 2, 512])
        rest = sb("e_rest", [P, 4, QUARTER // 4])
        found = sb("e_found", [P, 256])
        count = sb("e_count", [P, 256])
        signs = sb("e_signs", [P, NT])
        deg = sb("e_deg", [P, NT])
        off = sb("e_off", [P, NT])
        end = sb("e_end", [P, NT])
        full8 = sb("e_full8", [P, NT])
        aux = sb("e_aux", [P, 2, 3])
        absent = sb("e_absent", [P, NT, MAXC])
        began = sb("e_began", [P, MAXC])
        empty = sb("e_empty", [P, NT])
        sel_rows = sb("e_sel_rows", [P, plan.n_chunks * P])
        sel_edges = sb("e_sel_edges", [P, RING, P])
        slot_e = sb("e_slot_e", [P, 3, 512])
        spare = sb("e_spare", [P, 256])
        aux_e = sb("e_aux_e", [P, plan.n_chunks, 3])
        col_f = sb("e_col_f", [P, plan.n_chunks])
        col_i = sb("e_col_i", [P, plan.n_chunks], I32)
        starts = sb("e_starts", [P, plan.n_chunks, H])
        lasts = sb("e_lasts", [P, plan.n_chunks])
        ring = sb("e_ring", [P, RING, 2 * C])
        prod = sb("e_prod", [P, 2, 2 * C])
        score = sb("e_score", [P, 2, MAXC, H])
        turned = sb("e_turned", [P, 2 * P])
        run_max = sb("e_run_max", [P, P])
        last_max = sb("e_last_max", [P, MAXC, H])
        row_pen = sb("e_row_pen", [P, MAXC, H])
        row_max = sb("e_row_max", [P, H])
        shifted = sb("e_shifted", [P, MAXC, H])
        weight = sb("e_weight", [P, 2, MAXC, H])
        weighted = sb("e_weighted", [P, 3, 2 * C])
        empty_diag = sb("e_empty_diag", [P, P])
        rden = sb("e_rden", [P, H])
        y = sb("e_y", [P, C])
        neg_part = sb("e_neg_part", [P, C])
        stats = sb("e_stats", [P, 6])
        mv = sb("e_mv", [P, 2])
        lnv = sb("e_lnv", [P, 1])
        rstd = sb("e_rstd", [P, 1])
        y_out = sb("e_y_out", [P, 2, C])
        xt = sb("e_xt", [P, 2 * P])
        bad = sb("e_bad", [P, 3, NT])
        bad1 = sb("e_bad1", [P, 1])

        pv = [psum(f"e_pv{i}", [P, 512]) for i in range(2)]
        pg = [psum(f"e_pg{i}", [P, 512]) for i in range(2)]
        pq = [psum(f"e_pq{i}", [P, 512]) for i in range(2)]
        po = psum("e_po", [P, 512])
        pc = psum("e_pc", [P, 512])

        S = {}

        def s(name):
            if name not in S:
                S[name] = sem("e_" + name)
            return S[name]

        ring_loaded = [sem(f"e_ring_loaded{i}") for i in range(RING)]
        adj_loaded = [sem(f"e_adj_loaded{i}") for i in range(2)]
        out_stored = [sem(f"e_out_stored{i}") for i in range(2)]
        k_of = {t: k for k, t in enumerate(ORDER)}

        ahead = 2
        front, back = [], []
        for k in range(-ahead, NT):
            t = ORDER[k] if k >= 0 else None
            u = ORDER[k + ahead] if k + ahead < NT else None
            w = ORDER[k + 1] if 0 <= k + 1 < NT else None
            if t is not None:
                front.append(("score", 0, t))
            if u is not None:
                front.append(("extract", 0, u))
            if t is not None:
                front.append(("scan", 0, t))
            if u is not None:
                front.append(("place", 0, u))
            if t is not None:
                front += [("row_max", 0, t), ("shift", 0, t)]
                front.append(("weigh", 0, t))
            if u is not None:
                front.append(("list", 0, u))
            if t is not None:
                front.append(("finish", 0, t))
        back.append(("score", 1, ORDER[0]))
        for k in range(NT):
            t = ORDER[k]
            back += [("scan", 1, t)]
            if k + 1 < NT:
                back.append(("score", 1, ORDER[k + 1]))
            back += [("row_max", 1, t), ("shift", 1, t), ("weigh", 1, t), ("finish", 1, t)]

        def batch_no(layer, t, i):
            return layer * plan.n_batches + plan.batch0[t] + i

        def scan_no(layer, t, i):
            return layer * plan.n_scans + plan.scan0[t] + i

        def turn(layer, t):
            return layer * NT + k_of[t]

        def ring_at(t, c):
            return (plan.first[t] + c) % RING

        def arrived(eng, layer, t, c):
            q = layer * plan.n_chunks + plan.first[t] + c
            eng.wait_ge(ring_loaded[q % RING], 16 * (q // RING + 1))

        def at_least(eng, name, n):
            if n > 0:
                eng.wait_ge(s(name), n)

        def sel(t, c):
            q = plan.first[t] + c
            return sel_rows[:, q * P:(q + 1) * P]

        block = ctx.enter_context(nc.Block())

        @block.sync
        def _(sp):
            def load_adj(k):
                if k >= 2:
                    sp.wait_ge(s("sgn_ready"), k - 1)
                sp.dma_start(adj_tile[:, k % 2, :], adj[ORDER[k] * P:(ORDER[k] + 1) * P, :]).then_inc(adj_loaded[k % 2], 16)

            load_adj(0)
            load_adj(1)
            sp.dma_start(res[:], x.rearrange("(t p) c -> p t c", p=P)).then_inc(s("x_loaded"), 16)
            sp.dma_start(hx[:, :, 0:C], kv[:, C:2 * C].rearrange("(t p) c -> p t c", p=P)).then_inc(s("v_loaded"), 16)
            sp.dma_start(w_sb[:], w_nat.rearrange("(k p) c -> p k c", p=P)).then_inc(s("w_loaded"), 16)
            sp.dma_start(w_ext[:, :, 0:C], wT.rearrange("(k p) c -> p k c", p=P)).then_inc(s("w_loaded"), 16)
            sp.dma_start(b_row[:, 0:C], w_b.rearrange("(a c) -> a c", a=1)).then_inc(s("w_loaded"), 16)
            for o in range(2):
                sp.dma_start(b_col[:, o:o + 1], w_b[o * P:(o + 1) * P].rearrange("(p a) -> p a", a=1)).then_inc(s("w_loaded"), 16)
            sp.wait_ge(s("a_cleared"), 1)
            for h in range(H):
                rows = slice(h % 4 * D, h % 4 * D + D)
                sp.dma_start(a_diag[rows, h // 4, h:h + 1], a[D:2 * D, :]).then_inc(s("w_loaded"), 16)
                sp.dma_start(a_diag[rows, h // 4, H + h:H + h + 1], a[0:D, :]).then_inc(s("w_loaded"), 16)
            for k in range(2, NT):
                load_adj(k)
            for k, t in enumerate(ORDER):
                sp.wait_ge(s("h_ready"), k + 1)
                sp.dma_start(table[t * P:(t + 1) * P, :], hx[:, t, 0:CG]).then_inc(s("table_stored"), 16)
            for k, t in enumerate(ORDER):
                sp.wait_ge(s("out_ready"), k + 1)
                sp.dma_start(out[t * P:(t + 1) * P, :], y_out[:, k % 2, :]).then_inc(out_stored[k % 2], 16)
            for i in range(2):
                sp.wait_ge(out_stored[i], 16 * (NT // 2))

        @block.gpsimd
        def _(pool):
            n = Steps(pool, s("pool_step"))
            n.did(nc.gpsimd.memset(ident[:], 0.0))
            n.did(nc.gpsimd.memset(ones[:], 1.0))
            n.wait()
            nc.gpsimd.affine_select(out=ident[:], in_=ident[:], compare_op=ALU.not_equal, fill=1.0, base=0,
                                    pattern=[[-1, P]], channel_multiplier=1).then_inc(s("const_ready"), 1)
            pool.wait_ge(s("const_ready"), 1)
            nc.gpsimd.tensor_scalar(ident2048[:], ident[:], float(N), None, ALU.mult).then_inc(s("const_ready"), 1)
            nc.gpsimd.memset(ones_bf[:], 1.0).then_inc(s("const_ready"), 1)
            nc.gpsimd.iota(col_hi[:], pattern=[[4 * 64, QUARTER // 64]], base=0, channel_multiplier=0, allow_small_or_imprecise_dtypes=True).then_inc(s("const_ready"), 1)
            nc.gpsimd.iota(col_lo[:], pattern=[[1, 4], [4, 64]], base=0, channel_multiplier=0, allow_small_or_imprecise_dtypes=True).then_inc(s("const_ready"), 1)
            nc.gpsimd.affine_select(out=below[:], in_=ones[:], compare_op=ALU.is_gt, fill=0.0, base=0,
                                    pattern=[[1, P]], channel_multiplier=-1).then_inc(s("const_ready"), 1)
            nc.gpsimd.iota(edge_no[:], pattern=[[1, MAXC * P]], base=0, channel_multiplier=0, allow_small_or_imprecise_dtypes=True).then_inc(s("const_ready"), 1)
            nc.gpsimd.iota(row_no1[:], pattern=[[1, P]], base=1, channel_multiplier=0, allow_small_or_imprecise_dtypes=True).then_inc(s("const_ready"), 1)
            nc.gpsimd.iota(edge_no1[:], pattern=[[P, MAXC]], base=1, channel_multiplier=1, allow_small_or_imprecise_dtypes=True).then_inc(s("const_ready"), 1)
            nc.gpsimd.iota(chunk_at[:], pattern=[[P, MAXC + 1]], base=0, channel_multiplier=0, allow_small_or_imprecise_dtypes=True).then_inc(s("const_ready"), 1)
            nc.gpsimd.iota(part1[:], pattern=[[0, 1]], base=1, channel_multiplier=1, allow_small_or_imprecise_dtypes=True).then_inc(s("const_ready"), 1)
            nc.gpsimd.affine_select(out=is_tail[:], in_=ones[:, 0:1], compare_op=ALU.is_ge, fill=0.0, base=-(P - 1),
                                    pattern=[[0, 1]], channel_multiplier=1).then_inc(s("const_ready"), 1)
            nc.gpsimd.memset(mean_w[:], 1.0 / N).then_inc(s("const_ready"), 1)
            nc.gpsimd.memset(eps[:], EPS).then_inc(s("const_ready"), 1)
            nc.gpsimd.memset(mean_row[:, C:CG], 1.0).then_inc(s("const_ready"), 1)
            nc.gpsimd.memset(a_diag[:], 0.0).then_inc(s("a_cleared"), 1)
            for t in range(NT):
                nc.gpsimd.memset(caps[:, t:t + 1], float(P * CHUNKS[t])).then_inc(s("const_ready"), 1)

            def gather(layer, t, c, src, width):
                q = layer * plan.n_chunks + plan.first[t] + c
                if q >= RING:
                    pool.wait_ge(s("weighted_ready"), batch_of(q - RING) + 1)
                nc.gpsimd.indirect_dma_start(out=ring[:, q % RING, 0:width], out_offset=None, in_=src,
                                             in_offset=bass.IndirectOffsetOnAxis(ap=col_i[:, q % plan.n_chunks:q % plan.n_chunks + 1], axis=0)).then_inc(ring_loaded[q % RING], 16)

            def batch_of(q):
                layer, q = divmod(q, plan.n_chunks)
                t = [u for u in ORDER if plan.first[u] <= q][-1]
                c = q - plan.first[t]
                i = [i for i, (c0, n) in enumerate(plan.batches[t]) if c0 <= c][-1]
                return batch_no(layer, t, i)

            for t in ORDER:
                for r, (c0, m) in enumerate(plan.rounds[t]):
                    pool.wait_ge(s("index_ready"), plan.round0[t] + r + 1)
                    for c in range(c0, c0 + m):
                        gather(0, t, c, kv, 2 * C)
            pool.wait_ge(s("table_stored"), 16 * NT)
            for t in ORDER:
                for c in range(CHUNKS[t]):
                    gather(1, t, c, table, CG)

        @block.scalar
        def _(act):
            act.wait_ge(s("const_ready"), N_CONST)
            act.wait_ge(s("mean_summed"), 1)
            nc.scalar.copy(mean_row[:, 0:C], pq[0][:, 0:C]).then_inc(s("mean_ready"), 1)
            act.wait_ge(s("w_summed"), 1)
            for k in range(2):
                nc.scalar.copy(w_ext[:, k, C:CX], pq[1][:, k * 2 * H:(k + 1) * 2 * H]).then_inc(s("w_ready"), 1)
            nc.scalar.copy(b_row[:, C:CX], pq[1][0:1, 4 * H:6 * H]).then_inc(s("w_ready"), 1)

            for stage, layer, t in front + [("between", 1, 0)] + back:
                n = turn(layer, t)
                if stage == "extract":
                    k = k_of[t]
                    act.wait_ge(adj_loaded[k % 2], 16 * (k // 2 + 1))
                    at_least(act, "quarter_ready", 4 * (k - 1))
                    nc.scalar.activation(sgn[:, k % 2, :].rearrange("p (u i) -> p u i", u=4), adj_tile[:, k % 2, :].rearrange("p (i u) -> p u i", u=4), ACT.Sign, accum_out=signs[:, t:t + 1]).then_inc(s("sgn_ready"), 1)
                elif stage == "list":
                    for r, (c0, m) in enumerate(plan.rounds[t]):
                        at = plan.round0[t] + r
                        act.wait_ge(s("slots_moved"), at + 1)
                        at_least(act, "index_ready", at - 2)
                        w = m * 2 * plan.slots(t)
                        nc.scalar.copy(slot_e[:, at % 3, 0:w], pg[at % 2][:, 0:w]).then_inc(s("slots_copied"), 1)
                    act.wait_ge(s("aux_moved"), k_of[t] + 1)
                    C_t = CHUNKS[t]
                    nc.scalar.copy(aux_e[:, plan.first[t]:plan.first[t] + C_t, :].rearrange("p c k -> p (c k)"), pv[0][:, 0:3 * C_t]).then_inc(s("aux_copied"), 1)
                elif stage == "scan":
                    for g, (c0, m) in enumerate(plan.scans[t]):
                        at = scan_no(layer, t, g)
                        act.wait_ge(s("scores_turned"), at + 1)
                        at_least(act, "scanned", at)
                        nc.scalar.copy(turned[0:m * H, :], pc[0:m * H, 0:2 * P]).then_inc(s("turned_copied"), 1)
                elif stage == "shift":
                    act.wait_ge(s("shifted_ready"), n + 1)
                    at_least(act, "summed", n - 1)
                    nc.scalar.activation(weight[:, n % 2, 0:CHUNKS[t], :], shifted[:, 0:CHUNKS[t], :], ACT.Exp,
                                         scale=SCALE if layer == 0 else 1.0).then_inc(s("weight_ready"), 1)
                elif stage == "weigh":
                    at_least(act, "summed", n)
                    nc.scalar.activation(empty_diag[:], ident[:], ACT.Copy, scale=empty[:, t:t + 1]).then_inc(s("empty_ready"), 1)
                elif stage == "between":
                    act.wait_ge(s("mean_summed"), 2)
                    nc.scalar.copy(mean_row[:, 0:C], pq[0][:, 0:C]).then_inc(s("mean_ready"), 1)
                elif stage == "finish":
                    if layer == 1:
                        act.wait_ge(s("neg_ready"), k_of[t] + 1)
                        nc.scalar.activation(neg_part[:], neg_part[:], ACT.Exp).then_inc(s("elu_ready"), 1)
                    act.wait_ge(s("var_ready"), n + 1)
                    nc.scalar.activation(lnv[:], mv[:, 1:2], ACT.Ln, bias=eps[:]).then_inc(s("ln_ready"), 1)
                    act.wait_ge(s("ln_ready"), n + 1)
                    nc.scalar.activation(rstd[:], lnv[:], ACT.Exp, scale=-0.5).then_inc(s("rstd_ready"), 1)
                    if layer == 0:
                        act.wait_ge(s("norm_turned"), k_of[t] + 1)
                        nc.scalar.copy(xt[:], po[:, 0:2 * P]).then_inc(s("xt_ready"), 1)
                        act.wait_ge(s("h_summed"), k_of[t] + 1)
                        nc.scalar.copy(hx[:, t, :], po[:, 0:CX]).then_inc(s("h_ready"), 1)

        @block.tensor
        def _(pe):
            pe.wait_ge(s("const_ready"), N_CONST)
            pe.wait_ge(s("v_loaded"), 16)
            for t in range(NT):
                last = nc.tensor.matmul(pq[0][:, 0:C], mean_w[:], hx[:, t, 0:C], start=(t == 0), stop=(t == NT - 1))
            last.then_inc(s("mean_summed"), 1)
            pe.wait_ge(s("w_loaded"), 16 * (5 + 2 * H))
            for k in range(2):
                for o in range(2):
                    nc.tensor.matmul(pq[1][:, k * 2 * H:(k + 1) * 2 * H], w_sb[:, o, k * P:(k + 1) * P], a_diag[:, o, :], start=(o == 0), stop=(o == 1))
            for o in range(2):
                last = nc.tensor.matmul(pq[1][0:1, 4 * H:6 * H], b_col[:, o:o + 1], a_diag[:, o, :], start=(o == 0), stop=(o == 1))
            last.then_inc(s("w_summed"), 1)
            pe.wait_ge(s("x_loaded"), 16)

            for stage, layer, t in front + [("between", 1, 0)] + back:
                n = turn(layer, t)
                k = k_of[t]
                C_t = CHUNKS[t]
                if stage == "extract":
                    pe.wait_ge(s("sgn_ready"), k + 1)
                    for u in range(4):
                        at_least(pe, "quarter_read", 4 * k + u - 1)
                        if u < 2:
                            at_least(pe, ("aux_copied", "off_ready")[u], k)
                        cols = slice(u * QUARTER, (u + 1) * QUARTER)
                        nc.tensor.matmul(pv[u % 2][:], ident2048[:], sgn[:, k % 2, cols], start=True, stop=False)
                        nc.tensor.matmul(pv[u % 2][:], ones_bf[:], col_hi[:].unsqueeze(2).to_broadcast([1, QUARTER // 64, 64]), start=False, stop=False)
                        nc.tensor.matmul(pv[u % 2][:], ones_bf[:], col_lo[:, u:u + 1, :].to_broadcast([1, QUARTER // 64, 64]), start=False, stop=True).then_inc(s("quarter_ready"), 1)
                elif stage == "place":
                    pe.wait_ge(s("deg_ready"), k + 1)
                    nc.tensor.matmul(pv[1][:, 0:1], below[:], deg[:, t:t + 1], start=True, stop=True).then_inc(s("off_summed"), 1)
                elif stage == "list":
                    M2 = 2 * plan.slots(t)
                    pe.wait_ge(s("sel_ready"), k + 1)
                    for c in range(C_t):
                        last = nc.tensor.matmul(pv[0][:, 3 * c:3 * c + 3], sel(t, c), aux[:, k % 2, :], start=True, stop=True)
                    last.then_inc(s("aux_moved"), 1)
                    for r, (c0, m) in enumerate(plan.rounds[t]):
                        at = plan.round0[t] + r
                        at_least(pe, "slots_copied", at - 1)
                        for j in range(m):
                            last = nc.tensor.matmul(pg[at % 2][:, j * M2:(j + 1) * M2], sel(t, c0 + j), slot[:, k % 2, 0:M2], start=True, stop=True)
                        last.then_inc(s("slots_moved"), 1)
                elif stage == "score":
                    if layer == 0:
                        for i, (c0, m) in enumerate(plan.batches[t]):
                            b = batch_no(0, t, i)
                            at_least(pe, "queries_read", b - 1)
                            if b < 2:
                                pe.wait_ge(s("w_ready"), 3)
                                pe.wait_ge(s("mean_ready"), 1)
                            for j in range(m):
                                last = nc.tensor.matmul(pq[b % 2][:, j * C:(j + 1) * C], sel(t, c0 + j), res[:, t, :], start=True, stop=True)
                            last.then_inc(s("queries_moved"), 1)
                    else:
                        if k < 2:
                            pe.wait_ge(s("mean_ready"), 2)
                        at_least(pe, "src_read", k - 1)
                        for c in range(C_t):
                            last = nc.tensor.matmul(pq[k % 2][:, c * H:(c + 1) * H], sel(t, c), hx[:, t, CG:CX], start=True, stop=True)
                        last.then_inc(s("src_moved"), 1)
                elif stage == "scan":
                    for g, (c0, m) in enumerate(plan.scans[t]):
                        at = scan_no(layer, t, g)
                        pe.wait_ge(s("scores_ready"), n + 1)
                        if g == 0:
                            at_least(pe, "shifted_ready", n)
                        else:
                            pe.wait_ge(s("last_max_ready"), at)
                        q = plan.first[t] + c0
                        nc.tensor.transpose(pc[0:m * H, 0:P], starts[:, q:q + m, :].rearrange("p c h -> p (c h)"), ident[:])
                        nc.tensor.transpose(pc[0:m * H, P:2 * P], score[:, n % 2, c0:c0 + m, :].rearrange("p c h -> p (c h)"), ident[:]).then_inc(s("scores_turned"), 1)
                        pe.wait_ge(s("scanned"), at + 1)
                        nc.tensor.transpose(pc[:, 2 * P:2 * P + m * H], run_max[0:m * H, :], ident[0:m * H, 0:m * H]).then_inc(s("maxima_turned"), 1)
                elif stage == "row_max":
                    pe.wait_ge(s("last_max_ready"), scan_no(layer, t, 0) + len(plan.scans[t]))
                    if layer == 1:
                        pe.wait_ge(s("sel_edges_again"), k + 1)
                    for c in range(C_t):
                        last = nc.tensor.matmul(pc[:, c * H:(c + 1) * H], sel_edges[:, ring_at(t, c), :], last_max[:, c, :], start=True, stop=True)
                    last.then_inc(s("maxima_by_row"), 1)
                elif stage == "shift":
                    pe.wait_ge(s("row_max_ready"), n + 1)
                    for c in range(C_t):
                        last = nc.tensor.matmul(pc[:, 256 + c * H:256 + (c + 1) * H], sel(t, c), row_max[:], start=True, stop=True)
                    last.then_inc(s("maxima_by_edge"), 1)
                elif stage == "weigh":
                    if layer == 0:
                        at_least(pe, "h_ready", k)
                    else:
                        pe.wait_ge(s("h_ready"), NT)
                        at_least(pe, "sums_read", n)
                    pe.wait_ge(s("empty_ready"), n + 1)
                    nc.tensor.matmul(po[:, 0:CG], empty_diag[:], mean_row[:], start=True, stop=False, skip_group_check=True)
                    for i, (c0, m) in enumerate(plan.batches[t]):
                        pe.wait_ge(s("weighted_ready"), batch_no(layer, t, i) + 1)
                        for j in range(m):
                            c = c0 + j
                            e = sel_edges[:, ring_at(t, c), :]
                            nc.tensor.matmul(po[:, 0:C], e, weighted[:, batch_no(layer, t, i) % 3, j * C:(j + 1) * C], start=False, stop=False, skip_group_check=True)
                            last = nc.tensor.matmul(po[:, C:CG], e, weight[:, n % 2, c, :], start=False, stop=(c == C_t - 1), skip_group_check=True)
                        if i < len(plan.batches[t]) - 1:
                            last.then_inc(s("batch_summed"), 1)
                        else:
                            last.then_inc(s("summed"), 1)
                elif stage == "between":
                    pe.wait_ge(s("h_ready"), NT)
                    at_least(pe, "queries_read", plan.n_batches)
                    pe.wait_ge(s("summed"), NT)
                    for t in range(NT):
                        last = nc.tensor.matmul(pq[0][:, 0:C], mean_w[:], hx[:, t, 0:C], start=(t == 0), stop=(t == NT - 1))
                    last.then_inc(s("mean_summed"), 1)
                elif stage == "finish" and layer == 0:
                    pe.wait_ge(s("norm_ready"), k + 1)
                    for j in range(2):
                        last = nc.tensor.transpose(po[:, j * P:(j + 1) * P], res[:, t, j * P:(j + 1) * P], ident[:])
                    last.then_inc(s("norm_turned"), 1)
                    pe.wait_ge(s("xt_ready"), k + 1)
                    for j in range(2):
                        nc.tensor.matmul(po[:, 0:CX], xt[:, j * P:(j + 1) * P], w_ext[:, j, :], start=(j == 0), stop=False)
                    nc.tensor.matmul(po[:, 0:CX], ones[0:1, :], b_row[:], start=False, stop=True).then_inc(s("h_summed"), 1)
            pe.wait_ge(s("bad_ready"), 1)
            nc.tensor.matmul(pg[0][:, 0:1], ones[:], bad1[:], start=True, stop=True).then_inc(s("bad_summed"), 1)

        @block.vector
        def _(dve):
            v = nc.vector
            st = Steps(dve, s("dve_step"))
            dve.wait_ge(s("const_ready"), N_CONST)
            dve.wait_ge(s("x_loaded"), 16)

            def wait_summed(eng, b):
                layer, i = divmod(b, plan.n_batches)
                t = [u for u in ORDER if plan.batch0[u] <= i][-1]
                if i - plan.batch0[t] == len(plan.batches[t]) - 1:
                    eng.wait_ge(s("summed"), turn(layer, t) + 1)
                else:
                    eng.wait_ge(s("batch_summed"), b + 1 - turn(layer, t))

            def by_head(ap):
                return ap.rearrange("p (h d) -> p h d", d=D)

            for stage, layer, t in front + back:
                n = turn(layer, t)
                k = k_of[t]
                C_t = CHUNKS[t]
                q0 = plan.first[t]
                if stage == "extract":
                    M = plan.slots(t)
                    sq, R = SEGMENTS[t], ROUNDS[t]
                    if k >= 2:
                        u = ORDER[k - 2]
                        dve.wait_ge(s("slots_moved"), plan.round0[u] + len(plan.rounds[u]))
                    for u in range(4):
                        dve.wait_ge(s("quarter_ready"), 4 * k + u + 1)
                        segs = [pv[u % 2][:].rearrange("p (i g) -> p g i", g=sq)[:, g, :] for g in range(sq)]
                        to = [[slot[:, k % 2, M + ((u * sq + g) * R + r) * TOP:M + ((u * sq + g) * R + r + 1) * TOP] for r in range(R)] for g in range(sq)]
                        if R == 1:
                            for g in range(sq):
                                last = v.max(to[g][0], segs[g])
                            last.then_inc(s("quarter_read"), 1)
                        else:
                            for g in range(sq):
                                st.did(v.max(to[g][0], segs[g]))
                            st.wait()
                            for g in range(sq):
                                last = v.match_replace(rest[:, g, :], to[g][0], segs[g], 0.0)
                            last.then_inc(s("quarter_read"), 1)
                            dve.wait_ge(s("quarter_read"), 4 * k + u + 1)
                            for g in range(sq):
                                st.did(v.max(to[g][1], rest[:, g, :]))
                    dve.wait_ge(s("quarter_read"), 4 * k + 4)
                    st.wait()
                    vals = slot[:, k % 2, M:2 * M]
                    st.did(v.tensor_scalar(found[:, 0:M], vals, float(N), None, ALU.is_ge))
                    st.did(v.tensor_reduce(full8[:, t:t + 1], vals.rearrange("p (g r e) -> p g r e", r=R, e=TOP)[:, :, R - 1, TOP - 1], AX_X, ALU.max))
                    st.wait()
                    v.tensor_reduce(deg[:, t:t + 1], found[:, 0:M], AX_X, ALU.add).then_inc(s("deg_ready"), 1)
                    st.did(v.tensor_tensor_scan(count[:, 0:M], found[:, 0:M], found[:, 0:M], 0.0, ALU.add, ALU.max))
                elif stage == "place":
                    M = plan.slots(t)
                    dve.wait_ge(s("off_summed"), k + 1)
                    v.tensor_copy(off[:, t:t + 1], pv[1][:, 0:1]).then_inc(s("off_ready"), 1)
                    dve.wait_ge(s("off_ready"), k + 1)
                    dve.wait_ge(s("deg_ready"), k + 1)
                    st.wait()
                    st.did(v.tensor_tensor(end[:, t:t + 1], off[:, t:t + 1], deg[:, t:t + 1], ALU.add))
                    st.did(v.scalar_tensor_tensor(out=slot[:, k % 2, 0:M], in0=count[:, 0:M], scalar=off[:, t:t + 1], in1=found[:, 0:M], op0=ALU.add, op1=ALU.mult))
                    st.did(v.tensor_copy(aux[:, k % 2, 0:1], part1[:]))
                    st.did(v.tensor_scalar(aux[:, k % 2, 1:2], off[:, t:t + 1], 1.0, None, ALU.add))
                    st.did(v.tensor_scalar(empty[:, t:t + 1], deg[:, t:t + 1], 0.0, None, ALU.is_equal))
                    cols = sel_rows[:, q0 * P:(q0 + C_t) * P]
                    st.did(v.tensor_scalar(cols, edge_no[:, 0:C_t * P], off[:, t:t + 1], None, ALU.is_ge))
                    st.did(v.tensor_scalar(began[:, 0:C_t], chunk_at[:, 1:C_t + 1], off[:, t:t + 1], None, ALU.is_gt))
                    st.wait()
                    st.did(v.tensor_copy(aux[:, k % 2, 2:3], end[:, t:t + 1]))
                    st.did(v.scalar_tensor_tensor(out=absent[:, t, 0:C_t], in0=chunk_at[:, 0:C_t], scalar=end[:, t:t + 1], in1=began[:, 0:C_t], op0=ALU.is_lt, op1=ALU.mult))
                    st.wait()
                    st.did(v.tensor_scalar(absent[:, t, 0:C_t], absent[:, t, 0:C_t], -1.0, BIG, ALU.add, ALU.mult))
                    st.wait()
                    v.scalar_tensor_tensor(out=cols, in0=edge_no[:, 0:C_t * P], scalar=end[:, t:t + 1], in1=cols, op0=ALU.is_lt, op1=ALU.mult).then_inc(s("sel_ready"), 1)
                elif stage == "list":
                    M = plan.slots(t)
                    for r, (c0, m) in enumerate(plan.rounds[t]):
                        at = plan.round0[t] + r
                        dve.wait_ge(s("slots_copied"), at + 1)
                        for j in range(m):
                            c = c0 + j
                            st.wait()
                            st.did(v.scalar_tensor_tensor(out=spare[:, 0:M], in0=slot_e[:, at % 3, j * 2 * M:j * 2 * M + M], scalar=edge_no1[:, c:c + 1],
                                                          in1=slot_e[:, at % 3, j * 2 * M + M:(j + 1) * 2 * M], op0=ALU.is_equal, op1=ALU.mult, accum_out=col_f[:, q0 + c:q0 + c + 1]))
                        st.wait()
                        v.tensor_scalar(col_i[:, q0 + c0:q0 + c0 + m], col_f[:, q0 + c0:q0 + c0 + m], -float(N), 0.0, ALU.add, ALU.max).then_inc(s("index_ready"), 1)
                    dve.wait_ge(s("aux_copied"), k + 1)
                    row1, first1, end_e = (aux_e[:, q0:q0 + C_t, i] for i in range(3))
                    st.did(v.tensor_tensor(lasts[:, q0:q0 + C_t], end_e, edge_no1[:, 0:C_t], ALU.is_equal))
                    st.did(v.tensor_tensor(starts[:, q0:q0 + C_t, :], first1.unsqueeze(2).to_broadcast([P, C_t, H]), edge_no1[:, 0:C_t].unsqueeze(2).to_broadcast([P, C_t, H]), ALU.is_equal))
                    need = q0 + C_t - RING
                    if need > 0:
                        u = [u for u in ORDER if plan.first[u] < need][-1]
                        dve.wait_ge(s("summed"), turn(0, u) + 1)
                    for c in range(C_t):
                        st.did(v.tensor_scalar(sel_edges[:, ring_at(t, c), :], row_no1[:], aux_e[:, q0 + c, 0:1], None, ALU.is_equal))
                    st.wait()
                    st.did(v.tensor_scalar(lasts[:, q0:q0 + C_t], lasts[:, q0:q0 + C_t], is_tail[:], None, ALU.max))
                    st.did(v.tensor_scalar(starts[:, q0:q0 + C_t, :], starts[:, q0:q0 + C_t, :], -BIG, None, ALU.mult))
                    if k == NT - 1:
                        st.did(v.tensor_scalar(bad[:, 0, :], full8[:], float(N), None, ALU.is_ge))
                        st.did(v.tensor_tensor(bad[:, 1, :], end[:], caps[:], ALU.is_gt))
                        st.did(v.tensor_tensor(bad[:, 2, :], deg[:], signs[:], ALU.not_equal))
                        st.wait()
                        v.tensor_reduce(bad1[:], bad[:].rearrange("p a t -> p (a t)"), AX_X, ALU.add).then_inc(s("bad_ready"), 1)
                elif stage == "score" and layer == 0:
                    st.wait()
                    for i, (c0, m) in enumerate(plan.batches[t]):
                        b = batch_no(0, t, i)
                        at = ring_at(t, c0)
                        dve.wait_ge(s("queries_moved"), b + 1)
                        for j in range(m):
                            arrived(dve, 0, t, c0 + j)
                        st.wait()
                        v.tensor_tensor(prod[:, b % 2, 0:m * C].rearrange("p (c k) -> p c k", c=m), pq[b % 2][:, 0:m * C].rearrange("p (c k) -> p c k", c=m),
                                        ring[:, at:at + m, 0:C], ALU.mult).then_inc(s("queries_read"), 1)
                        dve.wait_ge(s("queries_read"), b + 1)
                        ins = v.tensor_reduce(score[:, n % 2, c0:c0 + m, :].rearrange("p c h -> p (c h)"), by_head(prod[:, b % 2, 0:m * C]), AX_X, ALU.add)
                        if i == len(plan.batches[t]) - 1:
                            ins.then_inc(s("scores_ready"), 1)
                        else:
                            st.did(ins)
                elif stage == "score":
                    dve.wait_ge(s("src_moved"), k + 1)
                    for c in range(C_t):
                        arrived(dve, 1, t, c)
                    c = 0
                    while c < C_t:
                        at = ring_at(t, c)
                        m = min(C_t - c, RING - at)
                        ins = v.tensor_tensor(score[:, n % 2, c:c + m, :], pq[k % 2][:, c * H:(c + m) * H].rearrange("p (c h) -> p c h", h=H), ring[:, at:at + m, C:CG], ALU.add)
                        c += m
                        if c < C_t:
                            st.did(ins)
                    ins.then_inc(s("src_read"), 1)
                    dve.wait_ge(s("src_read"), k + 1)
                    st.wait()
                    sc = score[:, n % 2, 0:C_t, :]
                    v.scalar_tensor_tensor(out=sc, in0=sc, scalar=SLOPE, in1=sc, op0=ALU.mult, op1=ALU.max).then_inc(s("scores_ready"), 1)
                    need = plan.n_chunks + q0 + C_t - RING
                    u = [u for u in ORDER if plan.n_chunks + plan.first[u] < need]
                    dve.wait_ge(s("summed"), turn(1, u[-1]) + 1 if u else NT)
                    for c in range(C_t):
                        last = v.tensor_scalar(sel_edges[:, ring_at(t, c), :], row_no1[:], aux_e[:, q0 + c, 0:1], None, ALU.is_equal)
                    last.then_inc(s("sel_edges_again"), 1)
                elif stage == "scan":
                    for g, (c0, m) in enumerate(plan.scans[t]):
                        at = scan_no(layer, t, g)
                        dve.wait_ge(s("turned_copied"), at + 1)
                        at_least(dve, "maxima_turned", at)
                        v.tensor_tensor_scan(run_max[0:m * H, :], turned[0:m * H, 0:P], turned[0:m * H, P:2 * P], -BIG, ALU.add, ALU.max).then_inc(s("scanned"), 1)
                        dve.wait_ge(s("maxima_turned"), at + 1)
                        at_least(dve, "maxima_by_row", n)
                        v.tensor_tensor(last_max[:, c0:c0 + m, :], pc[:, 2 * P:2 * P + m * H].rearrange("p (c h) -> p c h", h=H),
                                        lasts[:, q0 + c0:q0 + c0 + m].unsqueeze(2).to_broadcast([P, m, H]), ALU.mult).then_inc(s("last_max_ready"), 1)
                elif stage == "row_max":
                    dve.wait_ge(s("maxima_by_row"), n + 1)
                    st.wait()
                    st.did(v.tensor_tensor(row_pen[:, 0:C_t, :], pc[:, 0:C_t * H].rearrange("p (c h) -> p c h", h=H),
                                           absent[:, t, 0:C_t].unsqueeze(2).to_broadcast([P, C_t, H]), ALU.add))
                    st.wait()
                    at_least(dve, "maxima_by_edge", n)
                    v.tensor_reduce(row_max[:], row_pen[:, 0:C_t, :].rearrange("p c h -> p h c"), AX_X, ALU.max).then_inc(s("row_max_ready"), 1)
                elif stage == "shift":
                    dve.wait_ge(s("maxima_by_edge"), n + 1)
                    at_least(dve, "weight_ready", n)
                    dve.wait_ge(s("scores_ready"), n + 1)
                    v.tensor_tensor(shifted[:, 0:C_t, :], score[:, n % 2, 0:C_t, :], pc[:, 256:256 + C_t * H].rearrange("p (c h) -> p c h", h=H), ALU.subtract).then_inc(s("shifted_ready"), 1)
                elif stage == "weigh":
                    dve.wait_ge(s("weight_ready"), n + 1)
                    lo = C if layer == 0 else 0
                    for i, (c0, m) in enumerate(plan.batches[t]):
                        b = batch_no(layer, t, i)
                        at = ring_at(t, c0)
                        if b >= 3:
                            wait_summed(dve, b - 3)
                        v.tensor_tensor(weighted[:, b % 3, 0:m * C].rearrange("p (c h d) -> p c h d", c=m, d=D), ring[:, at:at + m, lo:lo + C].rearrange("p c (h d) -> p c h d", d=D),
                                        weight[:, n % 2, c0:c0 + m, :].unsqueeze(3).to_broadcast([P, m, H, D]), ALU.mult).then_inc(s("weighted_ready"), 1)
                elif stage == "finish":
                    dve.wait_ge(s("summed"), n + 1)
                    st.wait()
                    st.did(v.reciprocal(rden[:], po[:, C:CG]))
                    st.wait()
                    v.tensor_tensor(by_head(y[:]), by_head(po[:, 0:C]), rden[:].unsqueeze(2).to_broadcast([P, H, D]), ALU.mult).then_inc(s("sums_read"), 1)
                    dve.wait_ge(s("sums_read"), n + 1)
                    if layer == 0:
                        st.did(v.tensor_tensor(y[:], y[:], res[:, t, :], ALU.add))
                    else:
                        v.tensor_scalar(neg_part[:], y[:], 0.0, None, ALU.min).then_inc(s("neg_ready"), 1)
                        dve.wait_ge(s("elu_ready"), k + 1)
                        st.did(v.tensor_scalar(neg_part[:], neg_part[:], -1.0, None, ALU.add))
                        st.wait()
                        st.did(v.scalar_tensor_tensor(out=y[:], in0=y[:], scalar=0.0, in1=neg_part[:], op0=ALU.max, op1=ALU.add))
                        st.wait()
                        st.did(v.tensor_tensor(y[:], y[:], res[:, t, :], ALU.add))
                    st.wait()
                    st.did(v.bn_stats(stats[:], y[:]))
                    st.wait()
                    v.bn_aggr(mv[:], stats[:]).then_inc(s("var_ready"), 1)
                    dve.wait_ge(s("rstd_ready"), n + 1)
                    dve.wait_ge(s("var_ready"), n + 1)
                    if layer == 0:
                        v.tensor_scalar(res[:, t, :], y[:], mv[:, 0:1], rstd[:], ALU.subtract, ALU.mult).then_inc(s("norm_ready"), 1)
                        dve.wait_ge(s("norm_ready"), k + 1)
                    else:
                        if k >= 2:
                            dve.wait_ge(out_stored[k % 2], 16 * (k // 2))
                        v.tensor_scalar(y_out[:, k % 2, :], y[:], mv[:, 0:1], rstd[:], ALU.subtract, ALU.mult).then_inc(s("out_ready"), 1)
                        dve.wait_ge(s("out_ready"), k + 1)
            dve.wait_ge(s("bad_summed"), 1)
            v.tensor_scalar(needed, pg[0][0:1, 0:1], 0.0, None, ALU.is_gt)


N_CONST = 15 + 16


def resnorm_gnn(nc, x, xT, adj, kv, kT, v, w_nat, wT, w_b, a, out, table, sdT_dram):
    with nc.sbuf_tensor("needed", [1, 1], I32) as needed:
        edge_pass(nc, x, adj, kv, w_nat, wT, w_b, a, out, table, needed[:])
        general_pass(nc, x, xT, adj, kT, v, wT, w_b, a, out, sdT_dram, needed[:])


def kernel(x, adj, L0_gnn_x2, L0_gnn_v, L1_gnn_W_w, L1_gnn_W_b, L1_gnn_a):
    import numpy as np
    import concourse.bacc as bacc
    from concourse.bass_utils import run_bass_kernel_spmd

    nc = bacc.Bacc("TRN2", target_bir_lowering=False, num_devices=1)
    x, x2, v, w = (np.asarray(t) for t in (x, L0_gnn_x2, L0_gnn_v, L1_gnn_W_w))
    laid_out = {
        "x": x, "xT": x.T, "adj": adj, "kv": np.concatenate([x2, v], axis=1), "kT": x2.T, "v": v,
        "w_nat": w, "wT": w.T, "w_b": L1_gnn_W_b, "a": L1_gnn_a,
    }
    arrays, args = {}, []
    for name, arr in laid_out.items():
        arr = np.ascontiguousarray(arr)
        arrays[f"in_{name}"] = arr
        args.append(nc.dram_tensor(f"in_{name}", arr.shape, mybir.dt.from_np(arr.dtype), kind="ExternalInput").ap())
    N, C = x.shape
    args.append(nc.dram_tensor("out_0", x.shape, F32, kind="ExternalOutput").ap())
    args.append(nc.dram_tensor("table", (N, C + H), F32, kind="Internal").ap())
    args.append(nc.dram_tensor("sdT_dram", (H, N), F32, kind="Internal").ap())
    resnorm_gnn(nc, *args)
    return run_bass_kernel_spmd(nc, [arrays], core_ids=[0]).results[0]["out_0"]
```

```python
from contextlib import ExitStack

import concourse.bass as bass
from concourse import mybir

F32 = mybir.dt.float32
BF16 = mybir.dt.bfloat16
I32 = mybir.dt.int32
ALU = mybir.AluOpType
ACT = mybir.ActivationFunctionType
AX_X = mybir.AxisListType.X
ts = bass.ts

P = 128
H = 8
SLOPE = 0.2
EPS = 1e-5
NEG0 = 9000000000000000.0
NEG1 = 1000000000.0
STEPS = (1 + 3 * H + 5, 1 + 5 * H + 8)
ELU_AT = 1 + 5 * H + 1

BIG = 2.0 ** 100
TINY = 1e-30
TOP = 8
QUARTER = 512
RING = 20

CHUNKS = (16, 8, 6, 5, 5, 4, 4, 4, 4, 4, 3, 3, 3, 3, 3, 3)
SEGMENTS = (4,) + (2,) * 7 + (1,) * 8
ROUNDS = (2,) + (1,) * 15
ORDER = (15, 14, 12, 11, 1, 10, 9, 0, 8, 2, 7, 3, 6, 4, 5, 13)


class Steps:

    def __init__(self, eng, sem, base=0):
        self.eng, self.sem, self.base, self.n = eng, sem, base, 0

    def did(self, ins):
        ins.then_inc(self.sem, 1)
        self.n += 1

    def wait(self, but=0):
        self.eng.wait_ge(self.sem, self.base + self.n - but)




class Plan:

    def __init__(self):
        self.first, self.rounds, self.round0 = {}, {}, {}
        self.batches, self.batch0 = {}, {}
        q = r = 0
        for t in ORDER:
            self.first[t] = q
            per = 512 // (2 * self.slots(t))
            self.rounds[t] = [(c, min(per, CHUNKS[t] - c)) for c in range(0, CHUNKS[t], per)]
            self.round0[t] = r
            r += len(self.rounds[t])
            q += CHUNKS[t]
        self.n_chunks = q
        b = 0
        for layer in range(2):
            for t in ORDER:
                pairs, c = [], 0
                while c < CHUNKS[t]:
                    n = 2 if c + 1 < CHUNKS[t] and self.ring_at(layer, t, c) != RING - 1 else 1
                    pairs.append((c, n))
                    c += n
                self.batches[layer, t], self.batch0[layer, t] = pairs, b
                b += len(pairs)

    def slots(self, t):
        return 4 * SEGMENTS[t] * ROUNDS[t] * TOP

    def number(self, layer, t, c):
        return layer * self.n_chunks + self.first[t] + c

    def ring_at(self, layer, t, c):
        return self.number(layer, t, c) % RING


def general_pass(nc, x, xT, adj, kT, v, wT, w_b, a, out, sdT_dram, needed):
    N, C = x.shape
    D = C // H
    NT = N // P
    NB = N // 512
    SCALE = float(D) ** -0.5

    with ExitStack() as ctx:
        def sb(name, shape, dt=F32):
            return ctx.enter_context(nc.sbuf_tensor(name, shape, dt))

        def psum(name, shape):
            return ctx.enter_context(nc.psum_tensor(name, shape, F32))

        def sem(name):
            return ctx.enter_context(nc.semaphore(name))

        ident = sb("ident", [P, P])
        ones_row = sb("ones_row", [1, P])
        big = sb("big", [P, H, N])
        val = sb("val", [P, NT, C])
        res = sb("res", [P, NT, C])
        q_tile = sb("q_tile", [D, H, P])
        adj_tile = sb("adj_tile", [P, N], I32)
        mask = sb("mask", [P, N])
        fill = sb("fill", [P, N])
        score = sb("score", [P, N])
        prob = sb("prob", [P, N])
        probT = sb("probT", [P, NT, P])
        att = sb("att", [P, C])
        neg_part = sb("neg_part", [P, C])
        nmax = sb("nmax", [P, 1])
        rsum = sb("rsum", [P, 1])
        rinv = sb("rinv", [P, 1])
        mean = sb("mean", [P, 1])
        var = sb("var", [P, NT])
        std = sb("std", [P, NT])
        rstd = sb("rstd", [P, NT])
        wT_sb = sb("wT_sb", [P, 2, C])
        bias_row = sb("bias_row", [1, C])
        a_b = sb("a_b", [P, 2 * D])
        xt_sb = sb("xt_sb", [P, 2, P])
        ssrc = sb("ssrc", [P, NT, H])
        sdst = sb("sdst", [P, NT, H])
        sdT = sb("sdT", [H, N])

        ps_s = psum("ps_s", [P, N])
        ps_t = psum("ps_t", [P, 2, 512])
        ps_o = psum("ps_o", [P, 512])
        ps_m = psum("ps_m", [P, 512])

        const_ready = sem("const_ready")
        loaded = sem("loaded")
        layer1_loaded = sem("layer1_loaded")
        names = ["adj_loaded", "q_loaded", "adj_used", "q_used", "scores_ready", "scores_read", "pre_ready", "max_ready",
                 "probs_ready", "turned", "turn_copied", "summed", "att_ready", "exp_ready", "step", "var_ready", "std_ready"]
        S = [{n: sem(f"{n}{layer}") for n in names} for layer in range(2)]
        norm_ready = sem("norm_ready")
        xt_ready = sem("xt_ready")
        xt_copied = sem("xt_copied")
        h_ready = sem("h_ready")
        h_copied = sem("h_copied")
        hstep = sem("hstep")
        sd_turned = sem("sd_turned")
        sd_copied = sem("sd_copied")
        sd_stored = sem("sd_stored")
        out_done = sem("out_done")

        block = ctx.enter_context(nc.Block())

        @block.sync
        def _(sp):
            with sp.If(sp.value_load(needed, min_val=0, max_val=1) > 0):
                sp.dma_start(big[0:D, :, :], kT.rearrange("(h d) n -> d h n", d=D)).then_inc(loaded, 16)
                sp.dma_start(val[:], v.rearrange("(t p) c -> p t c", p=P)).then_inc(loaded, 16)
                sp.dma_start(res[:], x.rearrange("(t p) c -> p t c", p=P)).then_inc(loaded, 16)
                sp.dma_start(wT_sb[:], wT.rearrange("(k p) c -> p k c", p=P)).then_inc(loaded, 16)
                sp.dma_start(bias_row[:], w_b.rearrange("(a c) -> a c", a=1)).then_inc(loaded, 16)
                sp.dma_start(a_b[:], a.rearrange("k b -> b k").to_broadcast([P, 2 * D])).then_inc(loaded, 16)
                sp.wait_ge(sd_copied, NT)
                sp.wait_ge(norm_ready, 1)
                sp.dma_start(sdT_dram, sdT[:]).then_inc(sd_stored, 16)
                sp.wait_ge(sd_stored, 16)
                sp.dma_start(big[:], sdT_dram.rearrange("(a h) n -> a h n", a=1).to_broadcast([P, H, N])).then_inc(layer1_loaded, 16)
                sp.wait_ge(norm_ready, 2)
                sp.dma_start(out.rearrange("(t p) c -> p t c", p=P), res[:]).then_inc(out_done, 16)
                sp.wait_ge(out_done, 16)

        @block.gpsimd
        def _(pool):
            with pool.If(pool.value_load(needed, min_val=0, max_val=1) > 0):
                nc.gpsimd.memset(ident[:], 0.0).then_inc(const_ready, 1)
                pool.wait_ge(const_ready, 1)
                nc.gpsimd.affine_select(out=ident[:], in_=ident[:], compare_op=ALU.not_equal, fill=1.0, base=0,
                                        pattern=[[-1, P]], channel_multiplier=1).then_inc(const_ready, 1)
                nc.gpsimd.memset(ones_row[:], 1.0).then_inc(const_ready, 1)
                for layer in range(2):
                    s = S[layer]
                    if layer == 1:
                        pool.wait_ge(S[0]["adj_used"], NT + 1)
                    with pool.Fori(0, NT) as t:
                        pool.wait_ge(s["adj_used"], t + 1)
                        pool.dma_start(adj_tile[:], adj[ts(t, P), :]).then_inc(s["adj_loaded"], 16)
                        if layer == 0:
                            pool.wait_ge(s["q_used"], t + 1)
                            pool.dma_start(q_tile[:], xT[:, ts(t, P)].rearrange("(h d) n -> d h n", d=D)).then_inc(s["q_loaded"], 16)

        @block.tensor
        def _(pe):
            with pe.If(pe.value_load(needed, min_val=0, max_val=1) > 0):
                pe.wait_ge(const_ready, 3)
                pe.wait_ge(loaded, 96)
                for layer in range(2):
                    s = S[layer]
                    for name in ("turned", "summed"):
                        pe.sem_inc(s[name], 1)
                    if layer == 1:
                        pe.wait_ge(norm_ready, 1)
                        for t in range(NT):
                            if t >= 1:
                                pe.wait_ge(xt_copied, t)
                            for k in range(2):
                                last = nc.tensor.transpose(ps_t[:, 0, k * P:(k + 1) * P], res[:, t, k * P:(k + 1) * P], ident[:])
                            last.then_inc(xt_ready, 1)
                            pe.wait_ge(xt_copied, t + 1)
                            if t >= 1:
                                pe.wait_ge(h_copied, t)
                            for k in range(2):
                                nc.tensor.matmul(ps_m[:, 0:C], xt_sb[:, k, :], wT_sb[:, k, :], start=(k == 0), stop=False)
                            nc.tensor.matmul(ps_m[:, 0:C], ones_row[:], bias_row[:], start=False, stop=True).then_inc(h_ready, 1)
                        for t in range(NT):
                            pe.wait_ge(hstep, 4 * (t + 1))
                            if t >= 1:
                                pe.wait_ge(sd_copied, t)
                            nc.tensor.transpose(ps_o[0:H, 0:P], sdst[:, t, :], ident[:]).then_inc(sd_turned, 1)
                        pe.wait_ge(sd_copied, NT)
                    with pe.Fori(0, NT) as t:
                        for h in range(H):
                            n = t * H + h
                            if layer == 0:
                                if h == 0:
                                    pe.wait_ge(s["q_loaded"], 16 * t + 16)
                                pe.wait_ge(s["scores_read"], n + 1)
                                for b in range(NB):
                                    last = nc.tensor.matmul(ps_s[:, ts(b, 512)], q_tile[:, h, :], big[0:D, h, ts(b, 512)], start=True, stop=True)
                                last.then_inc(s["scores_ready"], 1)
                            pe.wait_ge(s["probs_ready"], n + 2)
                            for g in range(NT // 4):
                                pe.wait_ge(s["turn_copied"], 4 * n + max(g - 1, 0) + 1)
                                for j in range(4):
                                    last = nc.tensor.transpose(ps_t[:, g % 2, ts(j, P)], prob[:, ts(4 * g + j, P)], ident[:])
                                last.then_inc(s["turned"], 1)
                            pe.wait_ge(s["turn_copied"], 4 * n + 4 + 1)
                            if h == 0:
                                pe.wait_ge(s["att_ready"], t + 1)
                            for m in range(NT):
                                last = nc.tensor.matmul(ps_o[:, ts(h, D)], probT[:, m, :], val[:, m, ts(h, D)], start=(m == 0), stop=(m == NT - 1))
                            last.then_inc(s["summed"], 1)

        @block.scalar
        def _(act):
            with act.If(act.value_load(needed, min_val=0, max_val=1) > 0):
                for layer in range(2):
                    s = S[layer]
                    for name in ("turn_copied", "probs_ready"):
                        act.sem_inc(s[name], 1)
                    if layer == 1:
                        for t in range(NT):
                            act.wait_ge(xt_ready, t + 1)
                            if t >= 1:
                                act.wait_ge(h_ready, t)
                            nc.scalar.copy(xt_sb[:].rearrange("p k n -> p (k n)"), ps_t[:, 0, 0:2 * P]).then_inc(xt_copied, 1)
                            act.wait_ge(h_ready, t + 1)
                            nc.scalar.copy(val[:, t, :], ps_m[:, 0:C]).then_inc(h_copied, 1)
                        for t in range(NT):
                            act.wait_ge(sd_turned, t + 1)
                            nc.scalar.copy(sdT[:, ts(t, P)], ps_o[0:H, 0:P]).then_inc(sd_copied, 1)
                        act.wait_ge(layer1_loaded, 16)
                    with act.Fori(0, NT) as t:
                        for h in range(H):
                            n = t * H + h
                            if layer == 1:
                                act.wait_ge(s["turned"], 4 * n + 1)
                                nc.scalar.activation(prob[:], big[:, h, :], ACT.Identity, bias=ssrc[:, t, h:h + 1]).then_inc(s["pre_ready"], 1)
                            act.wait_ge(s["max_ready"], n + 1)
                            if layer == 0:
                                act.wait_ge(s["turned"], 4 * n + 1)
                            nc.scalar.activation(prob[:], score[:], ACT.Exp, bias=nmax[:], accum_out=rsum[:]).then_inc(s["probs_ready"], 1)
                            for g in range(NT // 4):
                                act.wait_ge(s["turned"], 4 * n + g + 2)
                                if g == 0:
                                    act.wait_ge(s["summed"], n + 1)
                                nc.scalar.copy(probT[:, ts(g, 4), :].rearrange("p m r -> p (m r)"), ps_t[:, g % 2, :]).then_inc(s["turn_copied"], 1)
                        if layer == 1:
                            act.wait_ge(s["step"], STEPS[1] * t + ELU_AT + 1)
                            nc.scalar.activation(neg_part[:], neg_part[:], ACT.Exp).then_inc(s["exp_ready"], 1)
                    act.wait_ge(s["var_ready"], 1)
                    nc.scalar.activation(std[:], std[:], ACT.Sqrt).then_inc(s["std_ready"], 1)

        @block.vector
        def _(dve):
            with dve.If(dve.value_load(needed, min_val=0, max_val=1) > 0):
                dve.wait_ge(loaded, 96)
                for layer in range(2):
                    s = S[layer]
                    for name in ("adj_used", "q_used", "scores_read", "att_ready", "step"):
                        dve.sem_inc(s[name], 1)
                    if layer == 1:
                        hs = Steps(dve, hstep)
                        for t in range(NT):
                            dve.wait_ge(h_copied, t + 1)
                            for k, dst in ((0, ssrc), (1, sdst)):
                                hs.wait()
                                hs.did(nc.vector.tensor_tensor(att[:].rearrange("p (h d) -> p h d", d=D), val[:, t, :].rearrange("p (h d) -> p h d", d=D),
                                                               a_b[:, k * D:(k + 1) * D].unsqueeze(1).to_broadcast([P, H, D]), ALU.mult))
                                hs.wait()
                                hs.did(nc.vector.tensor_reduce(dst[:, t, :], att[:].rearrange("p (h d) -> p h d", d=D), AX_X, ALU.add))
                    with dve.Fori(0, NT) as t:
                        st = Steps(dve, s["step"], STEPS[layer] * t + 1)
                        dve.wait_ge(s["adj_loaded"], 16 * (t + 1))
                        st.wait()
                        nc.vector.tensor_scalar(mask[:], adj_tile[:], 0.0, None, ALU.is_gt if layer == 0 else ALU.not_equal).then_inc(s["adj_used"], 1)
                        dve.wait_ge(s["adj_used"], t + 2)
                        st.did(nc.vector.tensor_scalar(fill[:], mask[:], -1.0, NEG0 if layer == 0 else NEG1, ALU.add, ALU.mult))
                        for h in range(H):
                            n = t * H + h
                            dve.wait_ge(s["probs_ready"], n + 1)
                            if layer == 0:
                                dve.wait_ge(s["scores_ready"], n + 1)
                                nc.vector.scalar_tensor_tensor(out=score[:], in0=ps_s[:], scalar=SCALE, in1=mask[:], op0=ALU.mult, op1=ALU.mult).then_inc(s["scores_read"], 1)
                                dve.wait_ge(s["scores_read"], n + 2)
                            else:
                                dve.wait_ge(s["pre_ready"], n + 1)
                                st.did(nc.vector.scalar_tensor_tensor(out=score[:], in0=prob[:], scalar=SLOPE, in1=prob[:], op0=ALU.mult, op1=ALU.max))
                                st.wait()
                                st.did(nc.vector.tensor_tensor(score[:], score[:], mask[:], ALU.mult))
                            st.wait()
                            st.did(nc.vector.tensor_tensor(score[:], score[:], fill[:], ALU.add))
                            st.wait()
                            nc.vector.tensor_reduce(nmax[:], score[:], AX_X, ALU.max, negate=True).then_inc(s["max_ready"], 1)
                            dve.wait_ge(s["probs_ready"], n + 2)
                            st.did(nc.vector.reciprocal(rinv[:], rsum[:]))
                            st.wait()
                            dve.wait_ge(s["summed"], n + 2)
                            st.did(nc.vector.tensor_scalar(att[:, ts(h, D)], ps_o[:, ts(h, D)], rinv[:], None, ALU.mult))
                        st.wait()
                        if layer == 0:
                            nc.vector.tensor_copy(mean[:], rinv[:]).then_inc(s["q_used"], 1)
                            dve.wait_ge(s["q_used"], t + 2)
                        if layer == 1:
                            st.did(nc.vector.tensor_scalar(neg_part[:], att[:], 0.0, None, ALU.min))
                            assert st.n == ELU_AT
                            dve.wait_ge(s["exp_ready"], t + 1)
                            st.did(nc.vector.tensor_scalar(neg_part[:], neg_part[:], -1.0, None, ALU.add))
                            st.wait()
                            st.did(nc.vector.scalar_tensor_tensor(out=att[:], in0=att[:], scalar=0.0, in1=neg_part[:], op0=ALU.max, op1=ALU.add))
                            st.wait()
                        st.did(nc.vector.tensor_tensor(att[:], res[:, t, :], att[:], ALU.add))
                        st.wait()
                        st.did(nc.vector.tensor_reduce(mean[:], att[:], AX_X, ALU.add))
                        st.wait()
                        st.did(nc.vector.tensor_scalar(mean[:], mean[:], 1.0 / C, None, ALU.mult))
                        st.wait()
                        st.did(nc.vector.tensor_scalar(res[:, t, :], att[:], mean[:], None, ALU.subtract))
                        st.wait()
                        st.did(nc.vector.tensor_tensor(att[:], res[:, t, :], res[:, t, :], ALU.mult))
                        st.wait()
                        nc.vector.tensor_reduce(var[:, ts(t, 1)], att[:], AX_X, ALU.add).then_inc(s["att_ready"], 1)
                        dve.wait_ge(s["att_ready"], t + 2)
                        assert st.n == STEPS[layer]
                    st = Steps(dve, s["step"], STEPS[layer] * NT + 1)
                    nc.vector.tensor_scalar(std[:], var[:], 1.0 / C, EPS, ALU.mult, ALU.add).then_inc(s["var_ready"], 1)
                    dve.wait_ge(s["std_ready"], 1)
                    st.did(nc.vector.reciprocal(rstd[:], std[:]))
                    st.wait()
                    for t in range(NT):
                        last = nc.vector.tensor_scalar(res[:, t, :], res[:, t, :], rstd[:, t:t + 1], None, ALU.mult)
                    last.then_inc(norm_ready, 1)




def edge_pass(nc, x, adj, kv, w_nat, wT, w_b, a, out, table, needed):
    N, C = x.shape
    D = C // H
    NT = N // P
    D1 = D + 1
    CV = H * D1
    CG = CV + H
    CX = CG + H
    SCALE = float(D) ** -0.5
    MAXC = max(CHUNKS)
    plan = Plan()

    with ExitStack() as ctx:
        def sb(name, shape, dt=F32):
            return ctx.enter_context(nc.sbuf_tensor(name, shape, dt))

        def psum(name, shape):
            return ctx.enter_context(nc.psum_tensor(name, shape, F32))

        def sem(name):
            return ctx.enter_context(nc.semaphore(name))

        ident = sb("e_ident", [P, P])
        ident2048 = sb("e_ident2048", [P, P], BF16)
        ones = sb("e_ones", [P, P])
        shift_up = sb("e_shift_up", [P, P])
        shift_down = sb("e_shift_down", [P, P])
        mean_w = sb("e_mean_w", [P, P])
        below = sb("e_below", [P, P])
        col_left = sb("e_col_left", [65, 4, P], BF16)
        col_right = sb("e_col_right", [65, QUARTER], BF16)
        edge_no = sb("e_edge_no", [P, MAXC * P])
        row_no1 = sb("e_row_no1", [P, P])
        edge_no1 = sb("e_edge_no1", [P, MAXC])
        chunk_no = sb("e_chunk_no", [P, MAXC, H])
        caps = sb("e_caps", [P, NT])
        part1 = sb("e_part1", [P, 1], BF16)
        minus_half = sb("e_minus_half", [P, 1])
        a_diag = sb("e_a_diag", [P, 2, 2 * H])
        w_ext = sb("e_w_ext", [P, 2, CX])
        b_row = sb("e_b_row", [1, CX])
        b_col = sb("e_b_col", [P, 2])
        x_parts = sb("e_x_parts", [P, NT, 3, C], BF16)
        res = x_parts[:].rearrange("p t k c -> p t (k c)")[:, :, 0:2 * C].bitcast(F32)
        x_tile = sb("e_x_tile", [P, 2, C])
        src_parts = sb("e_src_parts", [P, NT, 3, H], BF16)
        src_left = sb("e_src_left", [P, 2, H])
        hx = sb("e_hx", [P, NT, CX])
        mean_row = sb("e_mean_row", [P, C])
        node_sum = sb("e_node_sum", [P, CV])
        adj_tile = sb("e_adj", [P, 2, N], I32)
        sgn = sb("e_sgn", [P, 2, N], BF16)
        slot = sb("e_slot", [P, 2, 512])
        rest = sb("e_rest", [P, 4, QUARTER // 4])
        found = sb("e_found", [P, 256])
        count = sb("e_count", [P, 256])
        signs = sb("e_signs", [P, NT])
        deg = sb("e_deg", [P, NT])
        off = sb("e_off", [P, NT])
        end = sb("e_end", [P, NT])
        full8 = sb("e_full8", [P, NT])
        slot_hi = sb("e_slot_hi", [P, 2, 512], BF16)
        slot_lo = sb("e_slot_lo", [P, 2, 512], BF16)
        bounds = sb("e_bounds", [P, 2], I32)
        bound_chunk = sb("e_bound_chunk", [P, 2], I32)
        bound_at = sb("e_bound_at", [P, 2], I32)
        nonempty = sb("e_nonempty", [P, 1], I32)
        half_off = sb("e_half_off", [P, 1])
        pen_chunk = sb("e_pen_chunk", [P, 2, 2, MAXC * H], BF16)
        pen_at = sb("e_pen_at", [P, 2, 2, P], BF16)
        empty = sb("e_empty", [P, NT])
        sel_rows = sb("e_sel_rows", [P, plan.n_chunks * P], BF16)
        sel_edges = sb("e_sel_edges", [P, RING, P])
        slot_e = sb("e_slot_e", [P, 3, 512])
        spare = found
        row1_e = sb("e_row1_e", [P, plan.n_chunks])
        col_f = sb("e_col_f", [P, plan.n_chunks])
        col_i = sb("e_col_i", [P, plan.n_chunks], I32)
        pens = sb("e_pens", [P, NT, 2 * P], BF16)
        ring = sb("e_ring", [P, RING, C + CV])
        ring_flat = ring[:].rearrange("p r c -> p (r c)")
        x_full, left = (ring_flat[:, i * NT * C:(i + 1) * NT * C].rearrange("p (t c) -> p t c", c=C) for i in range(2))
        prod = sb("e_prod", [P, 2, 2 * C])
        score = sb("e_score", [P, 2, MAXC, H])
        turned = sb("e_turned", [P, 2, P])
        run = sb("e_run", [P, 3, P])
        top = sb("e_top", [P, P])
        shifted = sb("e_shifted", [P, P])
        weight_t = sb("e_weight_t", [P, P])
        weight = sb("e_weight", [P, 2, MAXC, H])
        weighted = sb("e_weighted", [P, 3, 2 * CV])
        w_sb = weighted[:].rearrange("p k c -> p (k c)")[:, 0:2 * C].rearrange("p (k c) -> p k c", c=C)
        empty_mean = sb("e_empty_mean", [P, C])
        den = sb("e_den", [P, H])
        rden = sb("e_rden", [P, H])
        y = sb("e_y", [P, C])
        neg_part = sb("e_neg_part", [P, C])
        stats = sb("e_stats", [P, 6])
        mv = sb("e_mv", [P, 2])
        var_eps = sb("e_var_eps", [P, 1])
        rstd = sb("e_rstd", [P, 1])
        shift = sb("e_shift", [P, 1])
        y_out = x_tile
        xt = neg_part
        bad = sb("e_bad", [P, 4, NT])
        bad1 = sb("e_bad1", [P, 1])

        pv = [psum(f"e_pv{i}", [P, 512]) for i in range(2)]
        pg = [psum(f"e_pg{i}", [P, 512]) for i in range(2)]
        pq = [psum(f"e_pq{i}", [P, 512]) for i in range(2)]
        po = psum("e_po", [P, 512])
        pc = psum("e_pc", [P, 512])

        S = {}

        def s(name):
            if name not in S:
                S[name] = sem("e_" + name)
            return S[name]

        ring_loaded = [sem(f"e_ring_loaded{i}") for i in range(RING)]
        adj_loaded = [sem(f"e_adj_loaded{i}") for i in range(2)]
        x_tile_loaded = [sem(f"e_x_tile_loaded{i}") for i in range(2)]
        out_stored = [sem(f"e_out_stored{i}") for i in range(2)]
        k_of = {t: k for k, t in enumerate(ORDER)}

        ahead = 2
        front, back = [], []
        for k in range(-ahead - 1, NT):
            p, t, following, u, v = (ORDER[i] if 0 <= i < NT else None for i in (k - 1, k, k + 1, k + ahead, k + ahead + 1))
            for stage, b in (("score_b", t), ("turn", t), ("scale_mean", t), ("scan", t), ("norm_c", p), ("quarter1", u), ("carry_up", t),
                             ("quarter2", u), ("carry_down", t), ("quarter3", u), ("move_pens", following), ("turn_norm", p), ("count", u), ("turn_back", t), ("place", u), ("project", p), ("select", u),
                             ("list_move", u), ("add_mean", t), ("make_pens", u), ("move_queries", following), ("weigh0", t), ("list", u), ("gather_a", u), ("score_a", following), ("weigh1", t), ("quarter0", v), ("weigh2", t), ("weigh3", t),
                             ("norm_a", t), ("norm_b", t), ("gather_b", u)):
                if b is not None:
                    front.append((stage, 0, b))
        front += [("norm_c", 0, ORDER[-1]), ("turn_norm", 0, ORDER[-1]), ("project", 0, ORDER[-1]), ("sum_h", 1, ORDER[0])]
        back += [("move_src", 1, ORDER[0]), ("move_src", 1, ORDER[1])]
        fetched = done = 0
        for k in range(-1, NT + 1):
            before, this, following, second = (ORDER[i] if 0 <= i < NT else None for i in (k - 1, k, k + 1, k + 2))
            fetches, edges = [], []
            while fetched < plan.n_chunks and fetched < done + RING:
                t = [u for u in ORDER if plan.first[u] <= fetched][-1]
                fetches.append(("fetch", t))
                fetched += 1
                if fetched == plan.first[t] + CHUNKS[t]:
                    edges.append(("turn_edges", t))
            if k < 0:
                back += [(stage, 1, b) for stage, b in fetches + edges]
                fetches, edges = [], []
            for stage, b in [("score", following), ("turn", following), ("weigh0", this)] + fetches + [("mean_h", this if k == 0 else None),
                             ("scan", following), ("norm_a", before), ("weigh1", this), ("carry_up", following), ("norm_b", before),
                             ("weigh2", this), ("carry_down", following), ("weigh3", this)] + edges + [("move_src", second if k >= 0 else None), ("turn_back", following), ("norm_c", before)]:
                if b is not None:
                    back.append((stage, 1, b))
            done += CHUNKS[this] if this is not None else 0

        def turn(layer, t):
            return layer * NT + k_of[t]

        def chunks_of(stage, t):
            i = int(stage[-1])
            return range(CHUNKS[t] * i // 4, CHUNKS[t] * (i + 1) // 4)

        def batch_of(layer, t, c):
            return [i for i, (c0, m) in enumerate(plan.batches[layer, t]) if c0 <= c][-1]

        def batches_of(stage, layer, t):
            ends = [max(3, batch_of(layer, t, CHUNKS[t] * (i + 1) // 4 - 1) + 1) if CHUNKS[t] * (i + 1) // 4 else 3 for i in range(4)]
            i = int(stage[-1])
            return list(enumerate(plan.batches[layer, t]))[ends[i - 1] if i else 0:ends[i]]

        def sums_of(layer, t):
            return pg[1] if layer == 1 and k_of[t] % 2 else po

        def batch_no(layer, t, i):
            return plan.batch0[layer, t] + i

        def arrived(eng, layer, t, c):
            q = plan.number(layer, t, c)
            eng.wait_ge(ring_loaded[q % RING], 16 * (q // RING + 1))

        def place_of(q):
            layer, i = divmod(q, plan.n_chunks)
            t = [u for u in ORDER if plan.first[u] <= i][-1]
            return layer, t, i - plan.first[t]

        def ring_summed(eng, layer, t):
            q = plan.number(layer, t, CHUNKS[t] - 1) - RING
            if q >= 0:
                before, u, _ = place_of(q)
                eng.wait_ge(s("summed"), turn(before, u) + 1)

        def groups(t):
            c = 0
            while c < CHUNKS[t]:
                at = plan.ring_at(1, t, c)
                m = min(4, CHUNKS[t] - c, RING - at)
                yield c, m, at
                c += m

        def group_no(t):
            return sum(len(list(groups(u))) for u in ORDER[:k_of[t]])

        def at_least(eng, name, n):
            if n > 0:
                eng.wait_ge(s(name), n)

        def sel(t, c):
            q = plan.first[t] + c
            return sel_rows[:, q * P:(q + 1) * P]

        block = ctx.enter_context(nc.Block())

        @block.sync
        def _(sp):
            def load_adj(k):
                if k >= 2:
                    sp.wait_ge(s("sgn_ready"), k - 1)
                sp.dma_start(adj_tile[:, k % 2, :], adj[ORDER[k] * P:(ORDER[k] + 1) * P, :]).then_inc(adj_loaded[k % 2], 16)

            def store_table(k):
                t = ORDER[k]
                sp.wait_ge(s("h_ready"), k + 1)
                sp.dma_start(table[t * P:(t + 1) * P, :], hx[:, t, 0:CG]).then_inc(s("table_stored"), 16)

            load_adj(0)
            load_adj(1)
            sp.dma_start(x_full, x.rearrange("(t p) c -> p t c", p=P)).then_inc(s("x_loaded"), 16)
            sp.dma_start(hx[:, :, 0:CV], kv[:, C:C + CV].rearrange("(t p) c -> p t c", p=P)).then_inc(s("v_loaded"), 16)
            sp.dma_start(w_sb, w_nat.rearrange("(k p) c -> p k c", p=P)).then_inc(s("w_loaded"), 16)
            for o in range(2):
                sp.dma_start(b_col[:, o:o + 1], w_b[o * P:(o + 1) * P].rearrange("(p a) -> p a", a=1)).then_inc(s("w_loaded"), 16)
            sp.wait_ge(s("cleared"), 4)
            for k in range(2):
                sp.dma_start(w_ext[:, k, 0:CV].rearrange("p (h e) -> p h e", e=D1)[:, :, 0:D], wT[k * P:(k + 1) * P, :].rearrange("p (h d) -> p h d", d=D)).then_inc(s("w_loaded"), 16)
            sp.dma_start(b_row[:, 0:CV].rearrange("p (h e) -> p h e", e=D1)[:, :, 0:D], w_b.rearrange("(a h d) -> a h d", a=1, d=D)).then_inc(s("w_loaded"), 16)
            for h in range(H):
                rows = slice(h % 4 * D, h % 4 * D + D)
                sp.dma_start(a_diag[rows, h // 4, h:h + 1], a[D:2 * D, :]).then_inc(s("w_loaded"), 16)
                sp.dma_start(a_diag[rows, h // 4, H + h:H + h + 1], a[0:D, :]).then_inc(s("w_loaded"), 16)
            load_adj(2)
            for k in range(NT + 2):
                if k < NT:
                    t = ORDER[k]
                    if k >= 2:
                        sp.wait_ge(s("x_tile_used"), k - 1)
                    sp.dma_start(x_tile[:, k % 2, :], x[t * P:(t + 1) * P, :]).then_inc(x_tile_loaded[k % 2], 16)
                if k + 3 < NT:
                    load_adj(k + 3)
                if k >= 2:
                    store_table(k - 2)
            for k, t in enumerate(ORDER):
                sp.wait_ge(s("normed"), NT + k + 1)
                sp.dma_start(out[t * P:(t + 1) * P, :], y_out[:, k % 2, :]).then_inc(out_stored[k % 2], 16)
            for i in range(2):
                sp.wait_ge(out_stored[i], 16 * (NT // 2))

        @block.gpsimd
        def _(pool):
            own = Steps(pool, s("pool_step"))
            own.did(nc.gpsimd.memset(ident[:], 0.0))
            own.did(nc.gpsimd.memset(ones[:], 1.0))
            own.did(nc.gpsimd.memset(col_left[:], 0.0))
            own.did(nc.gpsimd.memset(col_right[:], 0.0))
            own.wait()
            nc.gpsimd.affine_select(out=ident[:], in_=ident[:], compare_op=ALU.not_equal, fill=1.0, base=0,
                                    pattern=[[-1, P]], channel_multiplier=1).then_inc(s("const_ready"), 1)
            pool.wait_ge(s("const_ready"), 1)
            nc.gpsimd.tensor_scalar(ident2048[:], ident[:], float(N), None, ALU.mult).then_inc(s("const_ready"), 1)
            pool.wait_ge(s("const_ready"), 2)
            nc.gpsimd.memset(col_left[0:1], 1.0).then_inc(s("const_ready"), 1)
            pool.wait_ge(s("const_ready"), 3)
            nc.gpsimd.memset(col_left[32:33], 1.0).then_inc(s("const_ready"), 1)
            pool.wait_ge(s("const_ready"), 4)
            nc.gpsimd.iota(col_left[64:65], pattern=[[1, 4], [0, P]], base=0, channel_multiplier=0, allow_small_or_imprecise_dtypes=True).then_inc(s("const_ready"), 1)
            pool.wait_ge(s("const_ready"), 5)
            nc.gpsimd.iota(col_right[0:1], pattern=[[4 * 64, QUARTER // 64], [0, 64]], base=0, channel_multiplier=0, allow_small_or_imprecise_dtypes=True).then_inc(s("const_ready"), 1)
            pool.wait_ge(s("const_ready"), 6)
            nc.gpsimd.iota(col_right[32:33], pattern=[[0, QUARTER // 64], [4, 64]], base=0, channel_multiplier=0, allow_small_or_imprecise_dtypes=True).then_inc(s("const_ready"), 1)
            pool.wait_ge(s("const_ready"), 7)
            nc.gpsimd.memset(col_right[64:65], 1.0).then_inc(s("const_ready"), 1)
            pool.wait_ge(s("const_ready"), 8)
            nc.gpsimd.affine_select(out=below[:], in_=ones[:], compare_op=ALU.is_gt, fill=0.0, base=0,
                                    pattern=[[1, P]], channel_multiplier=-1).then_inc(s("const_ready"), 1)
            nc.gpsimd.iota(edge_no[:], pattern=[[1, MAXC * P]], base=0, channel_multiplier=0, allow_small_or_imprecise_dtypes=True).then_inc(s("const_ready"), 1)
            nc.gpsimd.iota(row_no1[:], pattern=[[1, P]], base=1, channel_multiplier=0, allow_small_or_imprecise_dtypes=True).then_inc(s("const_ready"), 1)
            nc.gpsimd.iota(edge_no1[:], pattern=[[P, MAXC]], base=1, channel_multiplier=1, allow_small_or_imprecise_dtypes=True).then_inc(s("const_ready"), 1)
            nc.gpsimd.iota(chunk_no[:], pattern=[[1, MAXC], [0, H]], base=0, channel_multiplier=0, allow_small_or_imprecise_dtypes=True).then_inc(s("const_ready"), 1)
            nc.gpsimd.iota(part1[:], pattern=[[0, 1]], base=1, channel_multiplier=1, allow_small_or_imprecise_dtypes=True).then_inc(s("const_ready"), 1)
            nc.gpsimd.affine_select(out=shift_up[:], in_=ones[:], compare_op=ALU.is_equal, fill=0.0, base=-H,
                                    pattern=[[1, P]], channel_multiplier=-1).then_inc(s("const_ready"), 1)
            nc.gpsimd.affine_select(out=shift_down[:], in_=ones[:], compare_op=ALU.is_equal, fill=0.0, base=H,
                                    pattern=[[1, P]], channel_multiplier=-1).then_inc(s("const_ready"), 1)
            nc.gpsimd.memset(mean_w[:], 1.0 / N).then_inc(s("const_ready"), 1)
            nc.gpsimd.memset(minus_half[:], -0.5).then_inc(s("const_ready"), 1)
            nc.gpsimd.memset(a_diag[:], 0.0).then_inc(s("cleared"), 1)
            nc.gpsimd.memset(w_ext[:, :, 0:CV], 0.0).then_inc(s("cleared"), 1)
            nc.gpsimd.memset(b_row[:, 0:CV], 0.0).then_inc(s("cleared"), 1)
            pool.wait_ge(s("cleared"), 3)
            nc.gpsimd.memset(b_row[:, 0:CV].rearrange("p (h e) -> p h e", e=D1)[:, :, D:D1], 1.0).then_inc(s("cleared"), 1)
            for t in range(NT):
                nc.gpsimd.memset(caps[:, t:t + 1], float(P * CHUNKS[t])).then_inc(s("const_ready"), 1)

            pool.wait_ge(s("x_part_ready"), 2)
            nc.gpsimd.tensor_tensor(x_parts[:, :, 2, :], left, x_parts[:, :, 1, :], ALU.subtract).then_inc(s("x_left_ready"), 1)
            pool.wait_ge(s("x_left_ready"), 2)

            def gather(layer, t, c, src, width):
                q = plan.number(layer, t, c)
                if q >= RING:
                    before, u, b = place_of(q - RING)
                    pool.wait_ge(s("weighted_ready"), batch_no(before, u, batch_of(before, u, b)) + 1)
                at = plan.first[t] + c
                nc.gpsimd.indirect_dma_start(out=ring[:, q % RING, 0:width], out_offset=None, in_=src,
                                             in_offset=bass.IndirectOffsetOnAxis(ap=col_i[:, at:at + 1], axis=0)).then_inc(ring_loaded[q % RING], 16)

            fetched = {}
            for stage, layer, t in front + back:
                n = turn(layer, t)
                if stage in ("gather_a", "gather_b"):
                    half = (CHUNKS[t] + 1) // 2
                    for r, (c0, m) in enumerate(plan.rounds[t]):
                        for c in range(c0, c0 + m):
                            if (c < half) == (stage == "gather_a"):
                                pool.wait_ge(s("index_ready"), plan.round0[t] + r + 1)
                                gather(0, t, c, kv, C + CV)
                if stage == "gather_b":
                    pool.wait_ge(s("row1_copied"), k_of[t] + 1)
                    ring_summed(pool, 0, t)
                    for c in range(CHUNKS[t]):
                        last = nc.gpsimd.tensor_scalar(sel_edges[:, plan.ring_at(0, t, c), :], row_no1[:], row1_e[:, plan.first[t] + c:plan.first[t] + c + 1], None, ALU.is_equal)
                    last.then_inc(s("sel_edges_ready"), 1)
                elif stage == "fetch":
                    pool.wait_ge(s("table_stored"), 16 * NT)
                    gather(1, t, fetched.get(t, 0), table, CG)
                    fetched[t] = fetched.get(t, 0) + 1
                elif stage == "make_pens":
                    k = k_of[t]
                    pool.wait_ge(s("bounds_ready"), 2 * k + 2)
                    at_least(pool, "pens_ready", k - 1)
                    for i in range(2):
                        CH = CHUNKS[t] * H
                        nc.gpsimd.tensor_scalar(pen_chunk[:, k % 2, i, 0:CH], chunk_no[:, 0:CHUNKS[t], :].rearrange("p c h -> p (c h)"), bound_chunk[:, i:i + 1], nonempty[:], ALU.is_equal, ALU.mult)
                        last = nc.gpsimd.tensor_scalar(pen_at[:, k % 2, i, :], edge_no[:, 0:P], bound_at[:, i:i + 1], -BIG, ALU.is_equal, ALU.mult)
                    last.then_inc(s("pens_made"), 1)
                elif stage == "add_mean":
                    k = k_of[t]
                    pool.wait_ge(x_tile_loaded[k % 2], 16 * (k // 2 + 1))
                    pool.wait_ge(s("mean_scaled"), k + 1)
                    nc.gpsimd.tensor_tensor(x_tile[:, k % 2, :], x_tile[:, k % 2, :], empty_mean[:], ALU.add).then_inc(s("residual_ready"), 1)
                elif stage == "norm_b":
                    pool.wait_ge(s("var_ready"), n + 1)
                    at_least(pool, "normed", n)
                    own.did(nc.gpsimd.tensor_scalar(var_eps[:], mv[:, 1:2], EPS, None, ALU.add))
                    own.wait()
                    own.did(nc.gpsimd.tensor_tensor(rstd[:], var_eps[:], minus_half[:], ALU.pow))
                    own.wait()
                    nc.gpsimd.tensor_scalar(shift[:], mv[:, 0:1], rstd[:], -1.0, ALU.mult, ALU.mult).then_inc(s("shift_ready"), 1)
                elif stage == "project":
                    src = hx[:, t, CG:CX]
                    pool.wait_ge(s("h_ready"), k_of[t] + 1)
                    own.did(nc.gpsimd.tensor_copy(src_parts[:, t, 0, :], src))
                    own.wait()
                    own.did(nc.gpsimd.tensor_tensor(src_left[:, 0, :], src, src_parts[:, t, 0, :], ALU.subtract))
                    own.wait()
                    own.did(nc.gpsimd.tensor_copy(src_parts[:, t, 1, :], src_left[:, 0, :]))
                    own.wait()
                    nc.gpsimd.tensor_tensor(src_parts[:, t, 2, :], src_left[:, 0, :], src_parts[:, t, 1, :], ALU.subtract).then_inc(s("src_parts_ready"), 1)

        @block.scalar
        def _(act):
            def copy_mean(bank):
                nc.scalar.copy(mean_row[:].rearrange("p (h d) -> p h d", d=D), bank[:, 0:CV].rearrange("p (h d) -> p h d", d=D1)[:, :, 0:D]).then_inc(s("mean_ready"), 1)

            def sign(k):
                t = ORDER[k]
                act.wait_ge(adj_loaded[k % 2], 16 * (k // 2 + 1))
                at_least(act, "quarter_ready", 4 * (k - 1))
                nc.scalar.activation(sgn[:, k % 2, :].rearrange("p (u i) -> p u i", u=4), adj_tile[:, k % 2, :].rearrange("p (i u) -> p u i", u=4), ACT.Sign, accum_out=signs[:, t:t + 1]).then_inc(s("sgn_ready"), 1)

            sign(0)
            sign(1)
            act.wait_ge(s("x_loaded"), 16)
            nc.scalar.copy(x_parts[:, :, 0, :], x_full).then_inc(s("x_part_ready"), 1)
            act.wait_ge(s("x_left_ready"), 1)
            nc.scalar.copy(x_parts[:, :, 1, :], left).then_inc(s("x_part_ready"), 1)
            act.wait_ge(s("mean_summed"), 1)
            copy_mean(pq[0])
            act.wait_ge(s("w_summed"), 1)
            for k in range(2):
                nc.scalar.copy(w_ext[:, k, CV:CX], pq[1][:, k * 2 * H:(k + 1) * 2 * H]).then_inc(s("w_ready"), 1)
            nc.scalar.copy(b_row[:, CV:CX], pq[1][0:1, 4 * H:6 * H]).then_inc(s("w_ready"), 1)

            for stage, layer, t in front + back:
                n = turn(layer, t)
                if stage == "list" and k_of[t] + 2 < NT:
                    sign(k_of[t] + 2)
                elif stage == "place":
                    act.wait_ge(s("half_off_ready"), k_of[t] + 1)
                    cols = slice(plan.first[t] * P, (plan.first[t] + CHUNKS[t]) * P)
                    nc.scalar.activation(sel_rows[:, cols], edge_no[:, 0:CHUNKS[t] * P], ACT.Sign, bias=half_off[:], scale=1.0).then_inc(s("from_off_ready"), 1)
                elif stage == "list_move":
                    for r, (c0, m) in enumerate(plan.rounds[t]):
                        at = plan.round0[t] + r
                        act.wait_ge(s("slots_moved"), at + 1)
                        at_least(act, "index_ready", at - 2)
                        w = m * 2 * plan.slots(t)
                        nc.scalar.copy(slot_e[:, at % 3, 0:w], pg[at % 2][:, 0:w]).then_inc(s("slots_copied"), 1)
                    C_t = CHUNKS[t]
                    act.wait_ge(s("rows_moved"), k_of[t] + 1)
                    nc.scalar.copy(row1_e[:, plan.first[t]:plan.first[t] + C_t], pv[0][:, 0:C_t]).then_inc(s("row1_copied"), 1)
                elif stage == "move_pens":
                    CH = CHUNKS[t] * H
                    act.wait_ge(s("pens_ready"), k_of[t] + 1)
                    nc.scalar.copy(pens[0:CH, t, :], pv[0][0:CH, 0:2 * P]).then_inc(s("pens_copied"), 1)
                elif stage == "turn":
                    act.wait_ge(s("scores_turned"), n + 1)
                    at_least(act, "shifted_ready", n - 1)
                    nc.scalar.copy(turned[0:CHUNKS[t] * H, n % 2, :], pc[0:CHUNKS[t] * H, 0:P]).then_inc(s("turned_copied"), 1)
                elif stage == "carry_down":
                    CH = CHUNKS[t] * H
                    act.wait_ge(s("shifted_ready"), n + 1)
                    at_least(act, "weight_turned", n)
                    nc.scalar.activation(weight_t[0:CH, :], shifted[0:CH, :], ACT.Exp, scale=SCALE if layer == 0 else 1.0).then_inc(s("exp_ready"), 1)
                elif stage == "turn_back":
                    CH = CHUNKS[t] * H
                    act.wait_ge(s("weight_turned"), n + 1)
                    if n >= 2:
                        before, u = divmod(n - 2, NT)
                        act.wait_ge(s("weighted_ready"), plan.batch0[before, ORDER[u]] + len(plan.batches[before, ORDER[u]]))
                    nc.scalar.copy(weight[:, n % 2, 0:CHUNKS[t], :].rearrange("p c h -> p (c h)"), pc[:, 2 * P:2 * P + CH]).then_inc(s("weight_ready"), 1)
                elif stage == "scale_mean":
                    act.wait_ge(s("mean_ready"), 1)
                    act.wait_ge(s("empty_ready"), k_of[t] + 1)
                    at_least(act, "residual_ready", k_of[t])
                    nc.scalar.activation(empty_mean[:], mean_row[:], ACT.Copy, scale=empty[:, t:t + 1]).then_inc(s("mean_scaled"), 1)
                elif stage == "mean_h":
                    act.wait_ge(s("mean_summed"), 2)
                    copy_mean(pg[0])
                elif stage == "turn_edges":
                    ring_summed(act, 1, t)
                    for g, (c, m, at) in enumerate(groups(t)):
                        act.wait_ge(s("edges_turned"), group_no(t) + g + 1)
                        last = nc.scalar.activation(sel_edges[:, at:at + m, :].rearrange("p c r -> p (c r)"), pv[(group_no(t) + g) % 2][:, 0:m * P], ACT.Copy, scale=1.0 / N).then_inc(s("edges_copied"), 1)
                elif stage == "norm_c":
                    act.wait_ge(s("shift_ready"), n + 1)
                    if layer == 0:
                        nc.scalar.activation(res[:, t, :], y[:], ACT.Identity, bias=shift[:], scale=rstd[:]).then_inc(s("normed"), 1)
                    else:
                        k = k_of[t]
                        if k >= 2:
                            act.wait_ge(out_stored[k % 2], 16 * (k // 2))
                        nc.scalar.activation(y_out[:, k % 2, :], y[:], ACT.Identity, bias=shift[:], scale=rstd[:]).then_inc(s("normed"), 1)
                elif stage == "norm_a" and layer == 1:
                    act.wait_ge(s("neg_ready"), k_of[t] + 1)
                    nc.scalar.activation(neg_part[:], neg_part[:], ACT.Exp).then_inc(s("elu_ready"), 1)
                elif stage == "turn_norm":
                    act.wait_ge(s("norm_turned"), k_of[t] + 1)
                    nc.scalar.copy(xt[:], po[:, 0:2 * P]).then_inc(s("xt_ready"), 1)
                elif stage == "project":
                    act.wait_ge(s("h_summed"), k_of[t] + 1)
                    nc.scalar.copy(hx[:, t, :], po[:, 0:CX]).then_inc(s("h_ready"), 1)

        @block.tensor
        def _(pe):
            pe.wait_ge(s("const_ready"), N_FIRST)

            def prepare():
                pe.wait_ge(s("const_ready"), N_CONST)
                pe.wait_ge(s("node_sum_ready"), 1)
                nc.tensor.matmul(pq[0][:, 0:CV], mean_w[:], node_sum[:], start=True, stop=True).then_inc(s("mean_summed"), 1)
                pe.wait_ge(s("w_loaded"), 16 * (6 + 2 * H))
                for k in range(2):
                    for o in range(2):
                        nc.tensor.matmul(pq[1][:, k * 2 * H:(k + 1) * 2 * H], w_sb[:, o, k * P:(k + 1) * P], a_diag[:, o, :], start=(o == 0), stop=(o == 1))
                for o in range(2):
                    last = nc.tensor.matmul(pq[1][0:1, 4 * H:6 * H], b_col[:, o:o + 1], a_diag[:, o, :], start=(o == 0), stop=(o == 1))
                last.then_inc(s("w_summed"), 1)

            for stage, layer, t in front + back:
                n = turn(layer, t)
                k = k_of[t]
                C_t = CHUNKS[t]
                if stage[:-1] == "quarter":
                    pe.wait_ge(s("sgn_ready"), k + 1)
                    for u in (int(stage[-1]),):
                        at_least(pe, "quarter_read", 4 * k + u - 1)
                        if u < 2:
                            at_least(pe, ("row1_copied", "off_ready")[u], k)
                        cols = slice(u * QUARTER, (u + 1) * QUARTER)
                        nc.tensor.matmul(pv[u % 2][:], ident2048[:], sgn[:, k % 2, cols], start=True, stop=False)
                        nc.tensor.matmul(pv[u % 2][:], col_left[:, u, :], col_right[:], start=False, stop=True).then_inc(s("quarter_ready"), 1)
                elif stage == "place":
                    if k == 0:
                        prepare()
                    M = plan.slots(t)
                    pe.wait_ge(s("count_ready"), k + 1)
                    nc.tensor.matmul(pv[1][:, 0:1], below[:], count[:, M - 1:M], start=True, stop=True).then_inc(s("off_summed"), 1)
                elif stage == "list_move":
                    M2 = 2 * plan.slots(t)
                    pe.wait_ge(s("sel_ready"), k + 1)
                    for r, (c0, m) in enumerate(plan.rounds[t]):
                        at = plan.round0[t] + r
                        at_least(pe, "slots_copied", at - 1)
                        for j in range(m):
                            for part in (slot_hi, slot_lo):
                                last = nc.tensor.matmul(pg[at % 2][:, j * M2:(j + 1) * M2], sel(t, c0 + j), part[:, k % 2, 0:M2], start=(part is slot_hi), stop=(part is slot_lo))
                        last.then_inc(s("slots_moved"), 1)
                    at_least(pe, "pens_copied", k)
                    for c in range(C_t):
                        last = nc.tensor.matmul(pv[0][:, c:c + 1], sel(t, c), part1[:], start=True, stop=True)
                    last.then_inc(s("rows_moved"), 1)
                elif stage == "move_pens":
                    pe.wait_ge(s("pens_made"), k + 1)
                    if k + 1 < NT:
                        pe.wait_ge(s("quarter_read"), 4 * (k + 1) + 3)
                    else:
                        pe.wait_ge(s("row1_copied"), NT)
                    for i in range(2):
                        last = nc.tensor.matmul(pv[0][0:C_t * H, i * P:(i + 1) * P], pen_chunk[:, k % 2, i, 0:C_t * H], pen_at[:, k % 2, i, :], start=True, stop=True)
                    last.then_inc(s("pens_ready"), 1)
                elif stage in ("move_queries", "score_b", "move_src"):
                    if layer == 0:
                        for i, (c0, m) in list(enumerate(plan.batches[0, t]))[slice(0, 2) if stage == "move_queries" else slice(2, None)]:
                            b = batch_no(0, t, i)
                            at_least(pe, "queries_read", b - 1)
                            if b < 2:
                                pe.wait_ge(s("w_ready"), 3)
                                pe.wait_ge(s("mean_ready"), 1)
                                pe.wait_ge(s("x_left_ready"), 2)
                            for j in range(m):
                                for part in range(3):
                                    last = nc.tensor.matmul(pq[b % 2][:, j * C:(j + 1) * C], sel(t, c0 + j), x_parts[:, t, part, :], start=(part == 0), stop=(part == 2))
                            last.then_inc(s("queries_moved"), 1)
                    else:
                        if k < 2:
                            pe.wait_ge(s("queries_read"), plan.batch0[1, ORDER[0]])
                            pe.wait_ge(s("src_parts_ready"), NT)
                        at_least(pe, "src_read", k - 1)
                        for c in range(C_t):
                            for part in range(3):
                                last = nc.tensor.matmul(pq[k % 2][:, c * H:(c + 1) * H], sel(t, c), src_parts[:, t, part, :], start=(part == 0), stop=(part == 2))
                        last.then_inc(s("src_moved"), 1)
                elif stage == "turn":
                    CH = C_t * H
                    pe.wait_ge(s("scores_ready"), n + 1)
                    at_least(pe, "weight_ready", n)
                    nc.tensor.transpose(pc[0:CH, 0:P], score[:, n % 2, 0:C_t, :].rearrange("p c h -> p (c h)"), ident[:]).then_inc(s("scores_turned"), 1)
                elif stage == "carry_up":
                    CH = C_t * H
                    pe.wait_ge(s("run_ready"), n + 1)
                    nc.tensor.matmul(pc[0:CH, P:P + 1], shift_up[0:CH, 0:CH], run[0:CH, 0, P - 1:P], start=True, stop=True).then_inc(s("carried_up"), 1)
                elif stage == "carry_down":
                    CH = C_t * H
                    pe.wait_ge(s("back_ready"), n + 1)
                    nc.tensor.matmul(pc[0:CH, P + 1:P + 2], shift_down[0:CH, 0:CH], run[0:CH, 2, 0:1], start=True, stop=True).then_inc(s("carried_down"), 1)
                elif stage == "turn_back":
                    CH = C_t * H
                    pe.wait_ge(s("exp_ready"), n + 1)
                    nc.tensor.transpose(pc[:, 2 * P:2 * P + CH], weight_t[0:CH, :], ident[0:CH, 0:CH]).then_inc(s("weight_turned"), 1)
                elif stage == "turn_edges":
                    if k == 0:
                        pe.wait_ge(s("row1_copied"), NT)
                        pe.wait_ge(s("pens_copied"), NT)
                        pe.wait_ge(s("off_ready"), NT)
                    for g, (c0, m, at) in enumerate(groups(t)):
                        number = group_no(t) + g
                        at_least(pe, "edges_copied", number - 1)
                        for j in range(m):
                            last = nc.tensor.matmul(pv[number % 2][:, j * P:(j + 1) * P], sel(t, c0 + j), ident2048[:], start=True, stop=True)
                        last.then_inc(s("edges_turned"), 1)
                elif stage[:5] == "weigh":
                    if layer == 0:
                        at_least(pe, "h_ready", k)
                        pe.wait_ge(s("sel_edges_ready"), k + 1)
                    else:
                        pe.wait_ge(s("h_ready"), NT)
                        pe.wait_ge(s("slots_copied"), sum(len(rounds) for rounds in plan.rounds.values()))
                        if k >= 2:
                            pe.wait_ge(s("sums_read"), n - 1)
                        pe.wait_ge(s("edges_copied"), group_no(t) + len(list(groups(t))))
                    for c in chunks_of(stage, t):
                        i = batch_of(layer, t, c)
                        c0, m = plan.batches[layer, t][i]
                        b = batch_no(layer, t, i)
                        pe.wait_ge(s("weighted_ready"), b + 1)
                        last = nc.tensor.matmul(sums_of(layer, t)[:, 0:CV], sel_edges[:, plan.ring_at(layer, t, c), :], weighted[:, b % 3, (c - c0) * CV:(c - c0 + 1) * CV], start=(c == 0), stop=(c == C_t - 1))
                        if c == C_t - 1:
                            last.then_inc(s("summed"), 1)
                        elif c == c0 + m - 1:
                            last.then_inc(s("batch_summed"), 1)
                elif stage == "mean_h":
                    pe.wait_ge(s("node_sum_ready"), 2)
                    nc.tensor.matmul(pg[0][:, 0:CV], mean_w[:], node_sum[:], start=True, stop=True).then_inc(s("mean_summed"), 1)
                elif stage == "turn_norm":
                    pe.wait_ge(s("normed"), k + 1)
                    for j in range(2):
                        last = nc.tensor.transpose(po[:, j * P:(j + 1) * P], res[:, t, j * P:(j + 1) * P], ident[:])
                    last.then_inc(s("norm_turned"), 1)
                elif stage == "project":
                    pe.wait_ge(s("xt_ready"), k + 1)
                    for j in range(2):
                        nc.tensor.matmul(po[:, 0:CX], xt[:, j * P:(j + 1) * P], w_ext[:, j, :], start=(j == 0), stop=False)
                    nc.tensor.matmul(po[:, 0:CX], ones[0:1, :], b_row[:], start=False, stop=True).then_inc(s("h_summed"), 1)
            pe.wait_ge(s("bad_ready"), 1)
            nc.tensor.matmul(pg[0][:, 0:1], ones[:], bad1[:], start=True, stop=True).then_inc(s("bad_summed"), 1)

        @block.vector
        def _(dve):
            v = nc.vector
            st = Steps(dve, s("dve_step"))

            def wait_summed(eng, b):
                layer, t = [lt for lt in plan.batch0 if plan.batch0[lt] <= b][-1]
                if b - plan.batch0[layer, t] == len(plan.batches[layer, t]) - 1:
                    eng.wait_ge(s("summed"), turn(layer, t) + 1)
                else:
                    eng.wait_ge(s("batch_summed"), b + 1 - turn(layer, t))

            def sum_nodes():
                v.tensor_reduce(node_sum[:], hx[:, :, 0:CV].rearrange("p t c -> p c t"), AX_X, ALU.add).then_inc(s("node_sum_ready"), 1)

            def by_head(ap):
                return ap.rearrange("p (h d) -> p h d", d=D)

            for stage, layer, t in front + back:
                n = turn(layer, t)
                k = k_of[t]
                C_t = CHUNKS[t]
                q0 = plan.first[t]
                M = plan.slots(t)
                sq, R = SEGMENTS[t], ROUNDS[t]
                if stage[:-1] == "quarter":
                    if k >= 2:
                        u = ORDER[k - 2]
                        dve.wait_ge(s("slots_moved"), plan.round0[u] + len(plan.rounds[u]))
                    for u in (int(stage[-1]),):
                        dve.wait_ge(s("quarter_ready"), 4 * k + u + 1)
                        segs = [pv[u % 2][:].rearrange("p (i g) -> p g i", g=sq)[:, g, :] for g in range(sq)]
                        to = [[slot[:, k % 2, M + ((u * sq + g) * R + r) * TOP:M + ((u * sq + g) * R + r + 1) * TOP] for r in range(R)] for g in range(sq)]
                        if R == 1:
                            for g in range(sq):
                                last = v.max(to[g][0], segs[g])
                            last.then_inc(s("quarter_read"), 1)
                        else:
                            for g in range(sq):
                                st.did(v.max(to[g][0], segs[g]))
                            st.wait()
                            for g in range(sq):
                                last = v.match_replace(rest[:, g, :], to[g][0], segs[g], 0.0)
                            last.then_inc(s("quarter_read"), 1)
                            dve.wait_ge(s("quarter_read"), 4 * k + u + 1)
                            for g in range(sq):
                                st.did(v.max(to[g][1], rest[:, g, :]))
                elif stage == "count":
                    dve.wait_ge(s("quarter_read"), 4 * k + 4)
                    st.wait()
                    vals = slot[:, k % 2, M:2 * M]
                    st.did(v.tensor_scalar(found[:, 0:M], vals, float(N), None, ALU.is_ge))
                    st.did(v.tensor_reduce(full8[:, t:t + 1], vals.rearrange("p (g r e) -> p g r e", r=R, e=TOP)[:, :, R - 1, TOP - 1], AX_X, ALU.max))
                    st.wait()
                    v.tensor_tensor_scan(count[:, 0:M], found[:, 0:M], found[:, 0:M], 0.0, ALU.add, ALU.max).then_inc(s("count_ready"), 1)
                    dve.wait_ge(s("count_ready"), k + 1)
                    st.did(v.tensor_copy(deg[:, t:t + 1], count[:, M - 1:M]))
                    if k == 0:
                        dve.wait_ge(s("x_part_ready"), 1)
                        v.tensor_tensor(left, x_full, x_parts[:, :, 0, :], ALU.subtract).then_inc(s("x_left_ready"), 1)
                        dve.wait_ge(s("v_loaded"), 16)
                        sum_nodes()
                        dve.wait_ge(s("const_ready"), N_CONST)
                elif stage == "sum_h":
                    dve.wait_ge(s("h_ready"), NT)
                    sum_nodes()
                elif stage == "place":
                    dve.wait_ge(s("off_summed"), k + 1)
                    v.tensor_copy(off[:, t:t + 1], pv[1][:, 0:1]).then_inc(s("off_ready"), 1)
                    dve.wait_ge(s("off_ready"), k + 1)
                    st.wait()
                    M2 = 2 * M
                    st.did(v.tensor_tensor(end[:, t:t + 1], off[:, t:t + 1], deg[:, t:t + 1], ALU.add))
                    st.did(v.scalar_tensor_tensor(out=slot[:, k % 2, 0:M], in0=count[:, 0:M], scalar=off[:, t:t + 1], in1=found[:, 0:M], op0=ALU.add, op1=ALU.mult))
                    v.tensor_scalar(half_off[:], off[:, t:t + 1], -1.0, 0.5, ALU.mult, ALU.add).then_inc(s("half_off_ready"), 1)
                    st.did(v.tensor_copy(bounds[:, 0:1], off[:, t:t + 1]))
                    v.tensor_scalar(empty[:, t:t + 1], deg[:, t:t + 1], 0.0, None, ALU.is_equal).then_inc(s("empty_ready"), 1)
                    at_least(dve, "pens_made", k)
                    st.did(v.tensor_scalar(nonempty[:], deg[:, t:t + 1], 0.0, None, ALU.is_gt))
                    st.wait()
                    st.did(v.tensor_copy(slot_hi[:, k % 2, 0:M2], slot[:, k % 2, 0:M2]))
                    st.did(v.tensor_scalar(bounds[:, 1:2], end[:, t:t + 1], -1.0, None, ALU.add))
                    st.wait()
                    st.did(v.tensor_tensor(slot_lo[:, k % 2, 0:M2], slot[:, k % 2, 0:M2], slot_hi[:, k % 2, 0:M2], ALU.subtract))
                    at_least(dve, "pens_made", k)
                    v.tensor_single_scalar(bound_chunk[:], bounds[:], 7, ALU.arith_shift_right).then_inc(s("bounds_ready"), 1)
                    v.tensor_single_scalar(bound_at[:], bounds[:], P - 1, ALU.bitwise_and).then_inc(s("bounds_ready"), 1)
                elif stage == "select":
                    cols = sel_rows[:, q0 * P:(q0 + C_t) * P]
                    st.wait()
                    dve.wait_ge(s("from_off_ready"), k + 1)
                    v.scalar_tensor_tensor(out=cols, in0=edge_no[:, 0:C_t * P], scalar=end[:, t:t + 1], in1=cols, op0=ALU.is_lt, op1=ALU.is_equal).then_inc(s("sel_ready"), 1)
                elif stage == "list":
                    M = plan.slots(t)
                    for r, (c0, m) in enumerate(plan.rounds[t]):
                        at = plan.round0[t] + r
                        dve.wait_ge(s("slots_copied"), at + 1)
                        for j in range(m):
                            c = c0 + j
                            half = j % 2 * M if M <= P else 0
                            st.wait(1 if j and M <= P else 0)
                            st.did(v.scalar_tensor_tensor(out=spare[:, half:half + M], in0=slot_e[:, at % 3, j * 2 * M:j * 2 * M + M], scalar=edge_no1[:, c:c + 1],
                                                          in1=slot_e[:, at % 3, j * 2 * M + M:(j + 1) * 2 * M], op0=ALU.is_equal, op1=ALU.mult, accum_out=col_f[:, q0 + c:q0 + c + 1]))
                        st.wait()
                        v.tensor_scalar(col_i[:, q0 + c0:q0 + c0 + m], col_f[:, q0 + c0:q0 + c0 + m], -float(N), 0.0, ALU.add, ALU.max).then_inc(s("index_ready"), 1)
                    if k == NT - 1:
                        st.did(v.tensor_scalar(bad[:, 0, :], full8[:], float(N), None, ALU.is_ge))
                        st.did(v.tensor_tensor(bad[:, 1, :], end[:], caps[:], ALU.is_gt))
                        st.did(v.tensor_tensor(bad[:, 2, :], deg[:], signs[:], ALU.not_equal))
                        st.did(v.tensor_scalar(bad[:, 3, :], deg[:], float(P), None, ALU.is_gt))
                        st.wait()
                        v.tensor_reduce(bad1[:], bad[:].rearrange("p a t -> p (a t)"), AX_X, ALU.add).then_inc(s("bad_ready"), 1)
                elif stage in ("score_a", "score_b"):
                    some = list(enumerate(plan.batches[layer, t]))
                    for pair in (some[i:i + 2] for i in ([0] if stage == "score_a" else range(2, len(some), 2))):
                        for i, (c0, m) in pair:
                            b = batch_no(0, t, i)
                            at = plan.ring_at(layer, t, c0)
                            dve.wait_ge(s("queries_moved"), b + 1)
                            for j in range(m):
                                arrived(dve, 0, t, c0 + j)
                            st.wait(1 if i >= 2 and i % 2 == 0 else 0)
                            v.tensor_tensor(prod[:, i % 2, 0:m * C].rearrange("p (c k) -> p c k", c=m), pq[b % 2][:, 0:m * C].rearrange("p (c k) -> p c k", c=m),
                                            ring[:, at:at + m, 0:C], ALU.mult).then_inc(s("queries_read"), 1)
                        for i, (c0, m) in pair:
                            dve.wait_ge(s("queries_read"), batch_no(0, t, i) + 1)
                            ins = v.tensor_reduce(score[:, n % 2, c0:c0 + m, :].rearrange("p c h -> p (c h)"), by_head(prod[:, i % 2, 0:m * C]), AX_X, ALU.add)
                            if i == len(some) - 1:
                                ins.then_inc(s("scores_ready"), 1)
                            else:
                                st.did(ins)
                elif stage == "score":
                    dve.wait_ge(s("src_moved"), k + 1)
                    for c in range(C_t):
                        arrived(dve, 1, t, c)
                    c = 0
                    while c < C_t:
                        at = plan.ring_at(layer, t, c)
                        m = min(C_t - c, RING - at)
                        ins = v.tensor_tensor(score[:, n % 2, c:c + m, :], pq[k % 2][:, c * H:(c + m) * H].rearrange("p (c h) -> p c h", h=H), ring[:, at:at + m, CV:CG], ALU.add)
                        c += m
                        if c < C_t:
                            st.did(ins)
                    ins.then_inc(s("src_read"), 1)
                    dve.wait_ge(s("src_read"), k + 1)
                    st.wait()
                    sc = score[:, n % 2, 0:C_t, :]
                    v.scalar_tensor_tensor(out=sc, in0=sc, scalar=SLOPE, in1=sc, op0=ALU.mult, op1=ALU.max).then_inc(s("scores_ready"), 1)
                elif stage == "scan":
                    CH = C_t * H
                    dve.wait_ge(s("turned_copied"), n + 1)
                    if layer == 0:
                        dve.wait_ge(s("pens_copied"), k + 1)
                    v.tensor_tensor_scan(run[0:CH, 0, :], pens[0:CH, t, 0:P], turned[0:CH, n % 2, :], -BIG, ALU.add, ALU.max).then_inc(s("run_ready"), 1)
                elif stage == "carry_up":
                    CH = C_t * H
                    dve.wait_ge(s("carried_up"), n + 1)
                    st.did(v.tensor_tensor_scan(run[0:CH, 1, :], pens[0:CH, t, 0:P], turned[0:CH, n % 2, :], pc[0:CH, P:P + 1], ALU.add, ALU.max))
                    st.wait()
                    v.tensor_tensor_scan(run[0:CH, 2, ::-1], pens[0:CH, t, P:2 * P][:, ::-1], run[0:CH, 1, ::-1], -BIG, ALU.add, ALU.max).then_inc(s("back_ready"), 1)
                elif stage == "carry_down":
                    CH = C_t * H
                    dve.wait_ge(s("carried_down"), n + 1)
                    st.did(v.tensor_tensor_scan(top[0:CH, ::-1], pens[0:CH, t, P:2 * P][:, ::-1], run[0:CH, 1, ::-1], pc[0:CH, P + 1:P + 2], ALU.add, ALU.max))
                    st.wait()
                    at_least(dve, "exp_ready", n)
                    v.tensor_tensor(shifted[0:CH, :], turned[0:CH, n % 2, :], top[0:CH, :], ALU.subtract).then_inc(s("shifted_ready"), 1)
                elif stage[:5] == "weigh":
                    dve.wait_ge(s("weight_ready"), n + 1)
                    if n == 0:
                        dve.wait_ge(s("w_ready"), 3)
                    lo = C if layer == 0 else 0
                    for i, (c0, m) in batches_of(stage, layer, t):
                        b = batch_no(layer, t, i)
                        at = plan.ring_at(layer, t, c0)
                        if b >= 3:
                            wait_summed(dve, b - 3)
                        v.tensor_tensor(weighted[:, b % 3, 0:m * CV].rearrange("p (c h d) -> p c h d", c=m, d=D1), ring[:, at:at + m, lo:lo + CV].rearrange("p c (h d) -> p c h d", d=D1),
                                        weight[:, n % 2, c0:c0 + m, :].unsqueeze(3).to_broadcast([P, m, H, D1]), ALU.mult).then_inc(s("weighted_ready"), 1)
                elif stage == "norm_a":
                    dve.wait_ge(s("summed"), n + 1)
                    sums = sums_of(layer, t)[:, 0:CV].rearrange("p (h d) -> p h d", d=D1)
                    st.did(v.tensor_scalar(den[:], sums[:, :, D], empty[:, t:t + 1], TINY, ALU.add, ALU.max))
                    st.wait()
                    st.did(v.reciprocal(rden[:], den[:]))
                    st.wait()
                    at_least(dve, "normed", n)
                    v.tensor_tensor(by_head(y[:]), sums[:, :, 0:D], rden[:].unsqueeze(2).to_broadcast([P, H, D]), ALU.mult).then_inc(s("sums_read"), 1)
                    dve.wait_ge(s("sums_read"), n + 1)
                    if layer == 0:
                        dve.wait_ge(s("residual_ready"), k + 1)
                        v.tensor_tensor(y[:], y[:], x_tile[:, k % 2, :], ALU.add).then_inc(s("x_tile_used"), 1)
                    else:
                        if k == 0:
                            dve.wait_ge(s("mean_ready"), 2)
                        st.did(v.scalar_tensor_tensor(out=y[:], in0=mean_row[:], scalar=empty[:, t:t + 1], in1=y[:], op0=ALU.mult, op1=ALU.add))
                        st.wait()
                        v.tensor_scalar(neg_part[:], y[:], 0.0, None, ALU.min).then_inc(s("neg_ready"), 1)
                elif stage == "norm_b":
                    if layer == 0:
                        dve.wait_ge(s("x_tile_used"), k + 1)
                    else:
                        dve.wait_ge(s("elu_ready"), k + 1)
                        st.wait()
                        st.did(v.scalar_tensor_tensor(out=y[:], in0=neg_part[:], scalar=-1.0, in1=y[:], op0=ALU.add, op1=ALU.max))
                        st.wait()
                        st.did(v.tensor_tensor(y[:], y[:], res[:, t, :], ALU.add))
                    st.wait()
                    st.did(v.bn_stats(stats[:], y[:]))
                    st.wait()
                    v.bn_aggr(mv[:], stats[:]).then_inc(s("var_ready"), 1)
            dve.wait_ge(s("bad_summed"), 1)
            v.tensor_scalar(needed, pg[0][0:1, 0:1], 0.0, None, ALU.is_gt)


N_FIRST = 8
N_CONST = 18 + 16


def resnorm_gnn(nc, x, xT, adj, kv, kT, v, w_nat, wT, w_b, a, out, table, sdT_dram):
    with nc.sbuf_tensor("needed", [1, 1], I32) as needed:
        edge_pass(nc, x, adj, kv, w_nat, wT, w_b, a, out, table, needed[:])
        general_pass(nc, x, xT, adj, kT, v, wT, w_b, a, out, sdT_dram, needed[:])


def kernel(x, adj, L0_gnn_x2, L0_gnn_v, L1_gnn_W_w, L1_gnn_W_b, L1_gnn_a):
    import numpy as np
    import concourse.bacc as bacc
    from concourse.bass_utils import run_bass_kernel_spmd

    nc = bacc.Bacc("TRN2", target_bir_lowering=False, num_devices=1)
    x, x2, v, w = (np.asarray(t) for t in (x, L0_gnn_x2, L0_gnn_v, L1_gnn_W_w))
    by_head = v.reshape(v.shape[0], H, -1)
    kv = np.concatenate([x2, np.concatenate([by_head, np.ones_like(by_head[:, :, :1])], axis=2).reshape(v.shape[0], -1)], axis=1)
    laid_out = {
        "x": x, "xT": x.T, "adj": adj, "kv": kv, "kT": x2.T, "v": v,
        "w_nat": w, "wT": w.T, "w_b": L1_gnn_W_b, "a": L1_gnn_a,
    }
    arrays, args = {}, []
    for name, arr in laid_out.items():
        arr = np.ascontiguousarray(arr)
        arrays[f"in_{name}"] = arr
        args.append(nc.dram_tensor(f"in_{name}", arr.shape, mybir.dt.from_np(arr.dtype), kind="ExternalInput").ap())
    N, C = x.shape
    args.append(nc.dram_tensor("out_0", x.shape, F32, kind="ExternalOutput").ap())
    args.append(nc.dram_tensor("table", (N, C + 2 * H), F32, kind="Internal").ap())
    args.append(nc.dram_tensor("sdT_dram", (H, N), F32, kind="Internal").ap())
    resnorm_gnn(nc, *args)
    return run_bass_kernel_spmd(nc, [arrays], core_ids=[0]).results[0]["out_0"]
```
